# Optimizing a Trainium2 kernel written in Bass

```python
import numpy as np
import jax
import jax.numpy as jnp

def _softmax(x, axis=-1):
    return jax.nn.softmax(x, axis=axis)
def _gelu(x):
    return jax.nn.gelu(x, approximate=True)
def _silu(x):
    return jax.nn.silu(x)
def _sigmoid(x):
    return jax.nn.sigmoid(x)
def _layernorm(x, axis=-1, eps=1e-5):
    m = jnp.mean(x, axis=axis, keepdims=True)
    v = jnp.var(x, axis=axis, keepdims=True)
    return (x - m) / jnp.sqrt(v + eps)
def _scatter_add(tgt, idx, src, axis=0):
    return tgt.at[idx].add(src)
def _segment_sum(src, seg, n):
    return jax.ops.segment_sum(src, seg, n)

kernel_name = 'mk_adj_resnorm_d2_adj_512_0deb7c'

def setup_inputs(seed: int = 0):
    np.random.seed(seed)
    _w = jnp.asarray
    def _rec_inputs():
        import jax
        import jax.numpy as jnp
        _gk = jax.random.key(seed)
        x = -0.0005207 + 1.001 * jax.random.normal(jax.random.fold_in(_gk, 1), (4096, 512), jnp.float32)
        _a = jax.random.bernoulli(jax.random.fold_in(_gk, 2), 0.00195312, (4096, 4096))
        _a = jnp.logical_or(_a, jnp.swapaxes(_a, -1, -2))
        _a = jnp.logical_or(_a, jnp.eye(4096, dtype=bool))
        adj = _a.astype(jnp.int32)
        return x, adj
    x, adj = _rec_inputs()
    def _L0_gnn_setup():
        import jax, jax.numpy as jnp
        import numpy as np
        ALPHA = 0.2
        NEG_FILL = -9000000000000000.0
        key = jax.random.key(seed)
        k1, k2, k3, k4 = jax.random.split(key, 4)
        N, D, H, F = (4096, 512, 8, 64)
        h = jax.random.normal(k1, (N, D), dtype=jnp.float32)
        adj = jax.random.randint(k2, (N, N), 0, 2, dtype=jnp.int32)
        W = jax.random.normal(k3, (H, D, F), dtype=jnp.float32) * (1.0 / np.sqrt(D))
        a = jax.random.normal(k4, (H, 2 * F), dtype=jnp.float32) * 0.1
        return {'h': h, 'adj': adj, 'W': W, 'a': a}
    _L0_gnn_all = _L0_gnn_setup()
    _L0_gnn_in = {k: v for k, v in _L0_gnn_all.items() if k in ('W', 'a', )}
    del _L0_gnn_all

    def _L1_gnn_setup():
        import jax, jax.numpy as jnp
        import numpy as np
        HEAD_SIZE = 8
        QK_DIM = 512
        V_DIM = 512
        N = 4096
        ATT_DIM = QK_DIM // HEAD_SIZE
        SCALE = ATT_DIM ** (-0.5)
        NEG_FILL = jnp.float32(-9000000000000000.0)
        key = jax.random.key(seed)
        k1, k2, k3, k4 = jax.random.split(key, 4)
        x1 = jax.random.normal(k1, (N, QK_DIM), dtype=jnp.float32)
        x2 = jax.random.normal(k2, (N, QK_DIM), dtype=jnp.float32)
        v = jax.random.normal(k3, (N, V_DIM), dtype=jnp.float32)
        adj = jax.random.randint(k4, (N, N), 0, 2, dtype=jnp.int32)
        return {'x1': x1, 'x2': x2, 'v': v, 'adj': adj}
    _L1_gnn_all = _L1_gnn_setup()
    _L1_gnn_in = {k: v for k, v in _L1_gnn_all.items() if k in ('x2', 'v', )}
    del _L1_gnn_all

    return {
        "x": x,
        "adj": adj,
        "L0_gnn_W": _L0_gnn_in["W"],
        "L0_gnn_a": _L0_gnn_in["a"],
        "L1_gnn_x2": _L1_gnn_in["x2"],
        "L1_gnn_v": _L1_gnn_in["v"],
    }

def reference(x, adj, L0_gnn_W, L0_gnn_a, L1_gnn_x2, L1_gnn_v):
    import jax
    import jax.numpy as jnp
    def _L0_gnn_ref(h, adj, W, a):
        import jax, jax.numpy as jnp
        import numpy as np
        ALPHA = 0.2
        NEG_FILL = -9000000000000000.0
        H, D, F = W.shape
        N = h.shape[0]
        hp = jnp.einsum('nd,hdf->hnf', h, W)
        a_src, a_dst = (a[:, :F], a[:, F:])
        f_src = jnp.einsum('hnf,hf->hn', hp, a_src)
        f_dst = jnp.einsum('hnf,hf->hn', hp, a_dst)
        e = jax.nn.leaky_relu(f_src[:, :, None] + f_dst[:, None, :], ALPHA)
        e = jnp.where(adj[None] > 0, e, NEG_FILL)
        att = jax.nn.softmax(e, axis=-1)
        out = jnp.einsum('hij,hjf->hif', att, hp)
        out = jnp.transpose(out, (1, 0, 2)).reshape(N, H * F)
        return jax.nn.elu(out)

    def _L1_gnn_ref(x1, x2, v, adj):
        import jax, jax.numpy as jnp
        import numpy as np
        HEAD_SIZE = 8
        QK_DIM = 512
        V_DIM = 512
        N = 4096
        ATT_DIM = QK_DIM // HEAD_SIZE
        SCALE = ATT_DIM ** (-0.5)
        NEG_FILL = jnp.float32(-9000000000000000.0)
        n = x1.shape[0]
        q = x1.reshape(n, HEAD_SIZE, -1).transpose(1, 0, 2) * SCALE
        k = x2.reshape(n, HEAD_SIZE, -1).transpose(1, 0, 2)
        vv = v.reshape(n, HEAD_SIZE, -1).transpose(1, 0, 2)
        scores = jnp.einsum('hnd,hmd->hnm', q, k)
        scores = jnp.where(adj > 0, scores, NEG_FILL)
        attn = jax.nn.softmax(scores, axis=-1)
        out = jnp.einsum('hnm,hmd->hnd', attn, vv)
        return out.transpose(1, 0, 2).reshape(n, -1)

    x = _layernorm(x + _L0_gnn_ref(x, adj, L0_gnn_W, L0_gnn_a), axis=-1)
    x = _layernorm(x + _L1_gnn_ref(x, L1_gnn_x2, L1_gnn_v, adj), axis=-1)
    return x


_drawn_inputs = setup_inputs


def setup_inputs(seed=0):
    import zlib

    import numpy as np

    out = dict(_drawn_inputs(seed))
    spreads = {}
    factors = {}
    for name, (base, spread) in spreads.items():
        noise = np.random.default_rng([zlib.crc32(name.encode()), seed]).standard_normal(out[name].shape)
        drawn = base * np.exp(spread * noise) if base else spread * noise
        out[name] = jnp.asarray(drawn.astype(out[name].dtype))
    for name, factor in factors.items():
        out[name] = (out[name] * factor).astype(out[name].dtype)
    return out
```

```python
from contextlib import ExitStack

import numpy as np

import concourse.bass as bass
from concourse import mybir

P = 128
ALU = mybir.AluOpType
ACT = mybir.ActivationFunctionType
F32 = mybir.dt.float32
F16 = mybir.dt.float16
BF16 = mybir.dt.bfloat16
I32 = mybir.dt.int32
AX_X = mybir.AxisListType.X
RMAX = bass.bass_isa.ReduceOp.max

SLOPE = 0.2
EPS = 1e-5
LOG_GAT_SCALE = float(10 * np.log(2.0))
LOG_ATT_SCALE = float(15 * np.log(2.0))
MASKED = -float(2.0**100)


def bass_gat_then_masked_attention(
    nc: bass.Bass,
    x: bass.AP,
    adj: bass.AP,
    W: bass.AP,
    a: bass.AP,
    x2: bass.AP,
    v: bass.AP,
    out: bass.AP,
):
    N, D = x.shape
    H, _, F = W.shape
    C = D // P
    NT = N // P
    SUB = 4
    IB = SUB * P
    NB = N // IB
    G = 4
    F1 = F + 1
    UW = 2 * F1
    RING = 4
    GROUPS = NT // 2
    SCALE = float(F) ** -0.5
    assert D == H * F and F == 64 and N % IB == 0 and H % 2 == 0 and NT == 32

    uw_d = nc.dram_tensor("uw_scratch", (H, P, NT, 2 * UW), F16, kind="Internal").ap()
    kT_d = nc.dram_tensor("kT_scratch", (H, P, N), F16, kind="Internal").ap()
    v_d = nc.dram_tensor("v_scratch", (H, P, NT, 2 * F1), F16, kind="Internal").ap()
    src_d = nc.dram_tensor("src_scratch", (H, N), F32, kind="Internal").ap()

    x_t = x.rearrange("(t p) d -> t p d", p=P)
    x2_t = x2.rearrange("(t p) d -> t p d", p=P)
    v_t = v.rearrange("(t p) d -> t p d", p=P)
    x_b = x.rearrange("(b s p) d -> b p s d", s=SUB, p=P)
    out_b = out.rearrange("(b s p) d -> b p s d", s=SUB, p=P)
    adj_b = adj.rearrange("(b s p) j -> b p s j", s=SUB, p=P)

    with ExitStack() as whole:

        def sb(stack, name, shape, dt):
            return stack.enter_context(nc.sbuf_tensor(name, shape, dt))

        def ps(stack, name, shape, dt):
            return stack.enter_context(nc.psum_tensor(name, shape, dt))

        def sem(stack, name):
            return stack.enter_context(nc.semaphore(name))

        ident = sb(whole, "ident", [P, P], F32)
        ident16 = sb(whole, "ident16", [P, P], F16)
        identb = sb(whole, "identb", [P, P], BF16)
        maskI = sb(whole, "maskI", [P, P], BF16)
        neg_dst = sb(whole, "neg_dst", [P, NT, H], F32)
        pos_w = sb(whole, "pos_w", [P, NT, H], F32)
        neg_w = sb(whole, "neg_w", [P, NT, H], F32)
        kmax2 = sb(whole, "kmax2", [P, H], F32)

        with ExitStack() as prep:
            Wsb = sb(prep, "Wsb", [P, C, D], F32)
            abc = sb(prep, "abc", [P, H, 2, F], F32)
            wprod = sb(prep, "wprod", [P, H, F], F32)
            Wa = sb(prep, "Wa", [P, C, 2, H], F32)
            hp_all = sb(prep, "hp_all", [P, NT, D], F32)
            x_s = sb(prep, "x_s", [P, G, D], F32)
            k_s = sb(prep, "k_s", [P, G, D], F32)
            v_s = sb(prep, "v_s", [P, G, D], F32)
            xT = sb(prep, "xT", [P, 2, D], F32)
            kk = sb(prep, "kk", [P, 2, H, 2, F], F16)
            kT_s = sb(prep, "kT_s", [P, 2, H, 2 * P], F16)
            vv = sb(prep, "vv", [P, 2, H, 2, 2 * F1], F16)
            ksq = sb(prep, "ksq", [P, 2, D], F32)
            kn2 = sb(prep, "kn2", [P, NT, H], F32)
            fT = sb(prep, "fT", [2 * H, N], F32)
            fall = sb(prep, "fall", [P, NT, 2, H], F32)
            mx = sb(prep, "mx", [P, 2, H], F32)
            amx = sb(prep, "amx", [P, 2, H], F32)
            zz = sb(prep, "zz", [P, NT, H], F32)
            mm = sb(prep, "mm", [P, NT, H], F32)
            dd = sb(prep, "dd", [P, NT, H], F32)
            ee = sb(prep, "ee", [P, NT, H, 2], F32)
            lgs = sb(prep, "lgs", [P, 1], F32)
            tw = sb(prep, "tw", [P, 2, H, 2, F1], F32)
            uws = sb(prep, "uws", [P, G, H, 2 * UW], F16)

            psT = [ps(prep, f"psT{i}", [P, 512], F32) for i in range(2)]
            psH = [ps(prep, f"psH{i}", [P, 512], F32) for i in range(2)]
            psK = [ps(prep, f"psK{i}", [P, H, P], F16) for i in range(2)]
            psF = ps(prep, "psF", [P, 512], F32)
            psD = ps(prep, "psD", [P, NT, 2 * H], F32)

            w_in = sem(prep, "w_in")
            ids = sem(prep, "ids")
            wa_chain = sem(prep, "wa_chain")
            wa_ready = sem(prep, "wa_ready")
            x_in = [sem(prep, f"x_in{i}") for i in range(G)]
            k_in = [sem(prep, f"k_in{i}") for i in range(G)]
            v_in = [sem(prep, f"v_in{i}") for i in range(G)]
            x_used = sem(prep, "x_used")
            k_used = sem(prep, "k_used")
            v_used = sem(prep, "v_used")
            xT_ps = sem(prep, "xT_ps")
            xT_sb = sem(prep, "xT_sb")
            fT_ps = sem(prep, "fT_ps")
            fT_sb = sem(prep, "fT_sb")
            hp_ps = sem(prep, "hp_ps")
            hp_sb = sem(prep, "hp_sb")
            khi = sem(prep, "khi")
            klo = sem(prep, "klo")
            ksq_done = sem(prep, "ksq_done")
            kn_done = sem(prep, "kn_done")
            kT_ps = sem(prep, "kT_ps")
            kT_sb = sem(prep, "kT_sb")
            kT_out = [sem(prep, f"kT_out{i}") for i in range(2)]
            vhi = sem(prep, "vhi")
            vlo = sem(prep, "vlo")
            v_ones = sem(prep, "v_ones")
            vv_out = [sem(prep, f"vv_out{i}") for i in range(2)]
            d_ps = sem(prep, "d_ps")
            d_sb = sem(prep, "d_sb")
            fmax = sem(prep, "fmax")
            amax = sem(prep, "amax")
            src_out = sem(prep, "src_out")
            ph = sem(prep, "ph")
            pool_held = sem(prep, "pool_held")
            ph_act = sem(prep, "ph_act")
            t_pos = sem(prep, "t_pos")
            t_neg = sem(prep, "t_neg")
            uw_hi = sem(prep, "uw_hi")
            uw_lo = sem(prep, "uw_lo")
            uw_out = [sem(prep, f"uw_out{i}") for i in range(G)]

            with nc.Block() as block:

                @block.sync
                def _(sp):
                    for c in range(C):
                        sp.dma_start(
                            Wsb[:, c, :].rearrange("p (h f) -> p h f", h=H),
                            W[:, c * P : (c + 1) * P, :].rearrange("h p f -> p h f"),
                        ).then_inc(w_in, 16)
                    sp.dma_start(
                        abc[:].rearrange("p h k f -> p (h k f)"),
                        a.rearrange("h f -> (h f)").partition_broadcast(P),
                    ).then_inc(w_in, 16)
                    with sp.Fori(0, NT // G) as g:
                        for k in range(G):
                            sp.wait_ge(x_used, g * G + k + 1)
                            sp.dma_start(x_s[:, k, :], x_t[bass.ds(g * G + k, 1)].rearrange("o p d -> p (o d)")).then_inc(x_in[k], 16)
                            sp.wait_ge(k_used, g * G + k + 1)
                            sp.dma_start(k_s[:, k, :], x2_t[bass.ds(g * G + k, 1)].rearrange("o p d -> p (o d)")).then_inc(k_in[k], 16)
                            sp.wait_ge(v_used, g * G + k + 1)
                            sp.dma_start(v_s[:, k, :], v_t[bass.ds(g * G + k, 1)].rearrange("o p d -> p (o d)")).then_inc(v_in[k], 16)
                            if k % 2 == 1:
                                i = k // 2
                                sp.wait_ge(kT_sb, g * G + k + 1 + 2)
                                sp.dma_start(
                                    kT_d[:, :, bass.ds((g * 2 + i) * 2 * P, 2 * P)].rearrange("h p n -> p h n"), kT_s[:, i]
                                ).then_inc(kT_out[i], 16)
                                sp.wait_ge(vlo, g * G + k + 1 + 2)
                                sp.dma_start(
                                    v_d[:, :, bass.ds((g * 2 + i) * 2, 2), :].rearrange("h p t c -> p h t c"), vv[:, i]
                                ).then_inc(vv_out[i], 16)
                    sp.wait_ge(fT_sb, NT + 1)
                    sp.dma_start(src_d, fT[0:H, :]).then_inc(src_out, 16)
                    with sp.Fori(0, NT // G) as g:
                        for k in range(G):
                            sp.wait_ge(uw_lo, g * G + k + 1 + 2)
                            sp.dma_start(
                                uw_d[:, :, bass.ds(g * G + k, 1), :].rearrange("h p o c -> p h (o c)"), uws[:, k]
                            ).then_inc(uw_out[k], 16)
                    for k in range(G):
                        sp.wait_ge(uw_out[k], 16 * (NT // G + 1))
                    for i in range(2):
                        sp.wait_ge(kT_out[i], 16 * (NT // G + 1))
                        sp.wait_ge(vv_out[i], 16 * (NT // G + 1))
                    sp.wait_ge(src_out, 16)

                @block.gpsimd
                def _(pool):
                    def hold(semaphore, value):
                        pool.wait_ge(semaphore, value)
                        pool.sem_inc(pool_held, 1)

                    nc.gpsimd.memset(ident[:], 0.0).then_inc(ids, 1)
                    nc.gpsimd.memset(vv[:], 0.0).then_inc(v_ones, 1)
                    pool.wait_ge(v_ones, 1)
                    nc.gpsimd.memset(vv[:, :, :, :, F : F + 1], 1.0).then_inc(v_ones, 1)
                    pool.wait_ge(ids, 1)
                    nc.gpsimd.affine_select(
                        out=ident[:], in_=ident[:], compare_op=ALU.not_equal, fill=1.0, base=0,
                        pattern=[[-1, P]], channel_multiplier=1,
                    ).then_inc(ids, 1)
                    pool.wait_ge(ids, 2)
                    nc.gpsimd.tensor_copy(ident16[:], ident[:]).then_inc(ids, 1)
                    nc.gpsimd.tensor_copy(identb[:], ident[:]).then_inc(ids, 1)
                    nc.gpsimd.tensor_scalar(maskI[:], ident[:], MASKED, None, ALU.mult).then_inc(ids, 1)
                    for i in range(2):
                        pool.sem_inc(vv_out[i], 16)
                    pool.sem_inc(v_used, G)
                    pool.sem_inc(vlo, 2)
                    pool.wait_ge(v_ones, 2)
                    with pool.Fori(0, NT // G) as g:
                        for k in range(G):
                            i, half = k // 2, k % 2
                            src = v_s[:, k, :].rearrange("p (h f) -> p h f", h=H)
                            hold(v_in[k], g * 16 + 16)
                            if half == 0:
                                hold(vv_out[i], g * 16 + 16)
                            nc.gpsimd.tensor_copy(vv[:, i, :, half, 0:F], src).then_inc(vhi, 1)
                            pool.wait_ge(vhi, g * G + k + 1)
                            nc.gpsimd.tensor_tensor(
                                vv[:, i, :, half, F1 : F1 + F], src, vv[:, i, :, half, 0:F], ALU.subtract
                            ).then_inc(vlo, 1)
                            hold(vlo, g * G + k + 3)
                            pool.sem_inc(v_used, 1)
                    pool.wait_ge(fmax, 2)
                    nc.gpsimd.partition_all_reduce(
                        amx[:].rearrange("p k h -> p (k h)"), mx[:].rearrange("p k h -> p (k h)"), P, RMAX
                    ).then_inc(amax, 1)
                    pool.wait_ge(ph_act, 4)
                    with pool.Fori(0, NT // 2) as g:
                        for i in range(2):
                            pool.wait_ge(uw_lo, g * 2 + i + 1)
                            nc.gpsimd.tensor_tensor(
                                tw[:, i, :, 1, 0:F],
                                hp_all[:, bass.ds(g * 2 + i, 1), :].rearrange("p o (h f) -> p (o h) f", h=H),
                                ee[:, bass.ds(g * 2 + i, 1), :, 1:2].rearrange("p o h k -> p (o h) k").to_broadcast([P, H, F]),
                                ALU.mult,
                            ).then_inc(t_neg, 1)

                @block.vector
                def _(dve):
                    for s_, n_ in ((x_used, 0), (k_used, G), (klo, 2), (kT_sb, 2), (fT_sb, 1)):
                        if n_:
                            dve.sem_inc(s_, n_)
                    nc.vector.memset(lgs[:], LOG_GAT_SCALE).then_inc(ph, 1)
                    dve.wait_ge(w_in, 16 * (C + 1))
                    n = 0
                    for c in range(C):
                        for k in range(2):
                            nc.vector.tensor_tensor(
                                wprod[:], Wsb[:, c, :].rearrange("p (h f) -> p h f", h=H), abc[:, :, k, :], ALU.mult
                            ).then_inc(wa_chain, 1)
                            n += 1
                            dve.wait_ge(wa_chain, n)
                            nc.vector.tensor_reduce(Wa[:, c, k, :], wprod[:], AX_X, ALU.add).then_inc(wa_chain, 1)
                            n += 1
                            dve.wait_ge(wa_chain, n)
                    dve.sem_inc(wa_ready, 1)
                    with dve.Fori(0, NT // G) as g:
                        for k in range(G):
                            i = k % 2
                            t1 = g * G + k + 1
                            dve.wait_ge(khi, t1)
                            nc.vector.tensor_tensor(
                                kk[:, i, :, 1, :], k_s[:, k, :].rearrange("p (h f) -> p h f", h=H), kk[:, i, :, 0, :], ALU.subtract
                            ).then_inc(klo, 1)
                            nc.vector.tensor_tensor(ksq[:, i, :], k_s[:, k, :], k_s[:, k, :], ALU.mult).then_inc(ksq_done, 1)
                            dve.wait_ge(ksq_done, t1)
                            dve.sem_inc(k_used, 1)
                            nc.vector.tensor_reduce(
                                kn2[:, bass.ds(g * G + k, 1), :].rearrange("p o h -> p (o h)"),
                                ksq[:, i, :].rearrange("p (h f) -> p h f", h=H), AX_X, ALU.add,
                            ).then_inc(kn_done, 1)
                            dve.wait_ge(fT_ps, t1)
                            nc.vector.tensor_copy(fT[:, bass.ds((g * G + k) * P, P)], psF[0 : 2 * H, 0:P]).then_inc(fT_sb, 1)
                    dve.wait_ge(d_ps, 1)
                    nc.vector.tensor_copy(fall[:].rearrange("p t k h -> p t (k h)"), psD[:]).then_inc(d_sb, 1)
                    dve.wait_ge(d_sb, 1)
                    dve.wait_ge(kn_done, NT)
                    nc.vector.tensor_reduce(mx[:, 0, :], fall[:, :, 1, :].rearrange("p t h -> p h t"), AX_X, ALU.max).then_inc(fmax, 1)
                    nc.vector.tensor_reduce(mx[:, 1, :], kn2[:].rearrange("p t h -> p h t"), AX_X, ALU.max).then_inc(fmax, 1)
                    nc.vector.tensor_scalar(neg_dst[:], fall[:, :, 1, :], -1.0, None, ALU.mult).then_inc(ph, 1)
                    dve.wait_ge(amax, 1)
                    top = amx[:, 0:1, :].to_broadcast([P, NT, H])
                    nc.vector.tensor_tensor(zz[:], fall[:, :, 0, :], top, ALU.add).then_inc(ph, 1)
                    nc.vector.tensor_tensor(dd[:], fall[:, :, 1, :], top, ALU.subtract).then_inc(ph, 1)
                    nc.vector.tensor_copy(kmax2[:], amx[:, 1, :]).then_inc(ph, 1)
                    dve.wait_ge(ph, 5)
                    nc.vector.scalar_tensor_tensor(mm[:], zz[:], SLOPE, zz[:], ALU.mult, ALU.max).then_inc(ph, 1)
                    dve.wait_ge(ph, 6)
                    nc.vector.tensor_tensor(pos_w[:], zz[:], mm[:], ALU.subtract).then_inc(ph, 1)
                    nc.vector.scalar_tensor_tensor(neg_w[:], zz[:], SLOPE, mm[:], ALU.mult, ALU.subtract).then_inc(ph, 1)
                    dve.wait_ge(ph_act, 4)
                    dve.sem_inc(uw_lo, 2)
                    dve.wait_ge(uw_lo, 2)
                    with dve.Fori(0, NT // G) as g:
                        for k in range(G):
                            i = k % 2
                            nc.vector.tensor_tensor(
                                tw[:, i, :, 0, 0:F],
                                hp_all[:, bass.ds(g * G + k, 1), :].rearrange("p o (h f) -> p (o h) f", h=H),
                                ee[:, bass.ds(g * G + k, 1), :, 0:1].rearrange("p o h k -> p (o h) k").to_broadcast([P, H, F]),
                                ALU.mult,
                            ).then_inc(t_pos, 1)
                            nc.vector.tensor_copy(
                                tw[:, i, :, :, F : F + 1].rearrange("p h k o -> p h (k o)"),
                                ee[:, bass.ds(g * G + k, 1), :, :].rearrange("p o h k -> p (o h) k"),
                            ).then_inc(t_pos, 1)
                            dve.wait_ge(uw_hi, g * G + k + 1)
                            nc.vector.tensor_tensor(
                                uws[:, k, :, UW : 2 * UW], tw[:, i].rearrange("p h k f -> p h (k f)"), uws[:, k, :, 0:UW], ALU.subtract
                            ).then_inc(uw_lo, 1)

                @block.scalar
                def _(act):
                    act.sem_inc(xT_sb, 2)
                    act.sem_inc(hp_sb, 2)
                    for i in range(2):
                        act.sem_inc(kT_out[i], 16)
                    for k in range(G):
                        act.sem_inc(uw_out[k], 16)
                    with act.Fori(0, NT // G) as g:
                        for k in range(G):
                            i = k % 2
                            t1 = g * G + k + 1
                            act.wait_ge(k_in[k], g * 16 + 16)
                            act.wait_ge(kT_ps, t1)
                            act.activation(kk[:, i, :, 0, :], k_s[:, k, :].rearrange("p (h f) -> p h f", h=H), ACT.Copy).then_inc(khi, 1)
                            act.wait_ge(xT_ps, t1)
                            act.activation(xT[:, i, :], psT[i][:], ACT.Copy).then_inc(xT_sb, 1)
                            act.wait_ge(hp_ps, t1)
                            act.activation(hp_all[:, bass.ds(g * G + k, 1), :].rearrange("p o d -> p (o d)"), psH[i][:], ACT.Copy).then_inc(hp_sb, 1)
                            act.wait_ge(kT_ps, t1 + 2)
                            if i == 0:
                                act.wait_ge(kT_out[k // 2], g * 16 + 16)
                            act.activation(kT_s[:, k // 2, :, i * P : (i + 1) * P], psK[i][:], ACT.Copy).then_inc(kT_sb, 1)
                    act.wait_ge(ph, 5)
                    act.activation(ee[:, :, :, 0:1].rearrange("p t h o -> p t (h o)"), dd[:], ACT.Exp, bias=lgs[:]).then_inc(ph_act, 1)
                    act.activation(ee[:, :, :, 1:2].rearrange("p t h o -> p t (h o)"), dd[:], ACT.Exp, bias=lgs[:], scale=SLOPE).then_inc(ph_act, 1)
                    act.wait_ge(ph, 8)
                    act.activation(pos_w[:], pos_w[:], ACT.Exp).then_inc(ph_act, 1)
                    act.activation(neg_w[:], neg_w[:], ACT.Exp).then_inc(ph_act, 1)
                    with act.Fori(0, NT // G) as g:
                        for k in range(G):
                            act.wait_ge(t_pos, (g * G + k) * 2 + 2)
                            act.wait_ge(t_neg, g * G + k + 1)
                            act.wait_ge(uw_out[k], g * 16 + 16)
                            act.activation(uws[:, k, :, 0:UW], tw[:, k % 2].rearrange("p h k f -> p h (k f)"), ACT.Copy).then_inc(uw_hi, 1)

                @block.tensor
                def _(pe):
                    pe.sem_inc(x_used, G)
                    pe.sem_inc(kT_ps, 2)
                    pe.wait_ge(ids, 5)
                    pe.wait_ge(wa_ready, 1)
                    with pe.Fori(0, NT // G) as g:
                        for k in range(G):
                            i = k % 2
                            t1 = g * G + k + 1
                            pe.wait_ge(x_in[k], g * 16 + 16)
                            pe.wait_ge(xT_sb, t1)
                            for c in range(C):
                                last = nc.tensor.transpose(psT[i][:, c * P : (c + 1) * P], x_s[:, k, c * P : (c + 1) * P], ident[:])
                            last.then_inc(xT_ps, 1)
                            pe.wait_ge(klo, t1 + 2)
                            pe.wait_ge(kT_sb, t1)
                            for h in range(H):
                                last = nc.tensor.transpose(psK[i][:, h, :], kk[:, i, h, :, :].rearrange("p k f -> p (k f)"), ident16[:])
                            last.then_inc(kT_ps, 1)
                            pe.wait_ge(xT_sb, t1 + 2)
                            pe.sem_inc(x_used, 1)
                            pe.wait_ge(hp_sb, t1)
                            for c in range(C):
                                last = nc.tensor.matmul(psH[i][:], xT[:, i, c * P : (c + 1) * P], Wsb[:, c, :], start=(c == 0), stop=(c == C - 1))
                            last.then_inc(hp_ps, 1)
                            pe.wait_ge(fT_sb, t1)
                            for c in range(C):
                                last = nc.tensor.matmul(
                                    psF[0 : 2 * H, 0:P], Wa[:, c, :, :].rearrange("p k h -> p (k h)"), xT[:, i, c * P : (c + 1) * P],
                                    start=(c == 0), stop=(c == C - 1),
                                )
                            last.then_inc(fT_ps, 1)
                    pe.wait_ge(fT_sb, NT + 1)
                    for t in range(NT):
                        last = nc.tensor.transpose(psD[:, t, :], fT[:, t * P : (t + 1) * P], ident[0 : 2 * H, 0 : 2 * H])
                    last.then_inc(d_ps, 1)

        with ExitStack() as main:
            adjT = sb(main, "adjT", [P, NT, IB], BF16)
            nmT = sb(main, "nmT", [P, NT, IB], BF16)
            adj_s = sb(main, "adj_s", [P, SUB, IB], I32)
            adj_n = sb(main, "adj_n", [P, SUB, IB], BF16)
            uw = sb(main, "uw", [P, 2, NT, 2 * UW], F16)
            src_bc = sb(main, "src_bc", [P, 2, IB], F32)
            dst_h = sb(main, "dst_h", [P, 2, NT], F32)
            mpos = sb(main, "mpos", [P, RING, IB], BF16)
            wall = sb(main, "wall", [P, 2, SUB, F1], F32)
            t1_ = sb(main, "t1_", [P, SUB, F1], F32)
            t2_ = sb(main, "t2_", [P, SUB, F1], F32)
            fac = sb(main, "fac", [P, 2, SUB, H], F32)
            rden = sb(main, "rden", [P, SUB], F32)
            X = sb(main, "X", [P, SUB, D], F32)
            O = sb(main, "O", [P, SUB, D], F32)
            E = sb(main, "E", [P, 2, 1024], F32)
            qq = sb(main, "qq", [P, SUB, H, 3, F], F16)
            qT = sb(main, "qT", [P, 2, 2, IB], F16)
            phi = sb(main, "phi", [P, 2, 1024], F16)
            plo = sb(main, "plo", [P, 2, 1024], F16)
            kT = sb(main, "kT", [P, 2, N], F16)
            vs = sb(main, "vs", [P, 2, NT, 2 * F1], F16)
            stats = sb(main, "stats", [P, SUB, 6], F32)
            mv = sb(main, "mv", [P, SUB, 2], F32)
            rstd = sb(main, "rstd", [P, SUB], F32)
            mhalf = sb(main, "mhalf", [P, SUB], F32)
            phalf = sb(main, "phalf", [P, H], F32)
            qn2 = sb(main, "qn2", [P, SUB, H], F32)
            qm = sb(main, "qm", [P, H], F32)
            qam = sb(main, "qam", [P, H], F32)
            qk2 = sb(main, "qk2", [P, H], F32)
            shift = sb(main, "shift", [P, H], F32)
            shift_h = sb(main, "shift_h", [P, 2, 1], F32)
            Ef = E[:].rearrange("p a b -> p (a b)")
            Xf = X[:].rearrange("p s d -> p (s d)")
            Of = O[:].rearrange("p s d -> p (s d)")

            ps_all = ps(main, "ps_all", [P, 8, 512], F32)
            psU = [ps_all[:, 2 * i : 2 * i + 2, 0 : 2 * UW].rearrange("p b (s c) -> p b s c", s=2) for i in range(2)]
            psW = [ps_all[:, 4 + i, 0 : SUB * F1].rearrange("p (s c) -> p s c", s=SUB) for i in range(2)]
            psS = [ps_all[:, 2 * i : 2 * i + 2, :].rearrange("p b n -> p (b n)") for i in range(2)]
            psO = psW
            psA = ps_all[:, 6, :].bitcast(BF16).rearrange("p (t s n) -> p t s n", t=2, s=SUB)
            psQ = ps_all[:, 7, :].bitcast(F16).rearrange("p (k n) -> p k n", k=2)

            adj_in = sem(main, "adj_in")
            adj_free = sem(main, "adj_free")
            adjn_ready = sem(main, "adjn_ready")
            adjn_read = sem(main, "adjn_read")
            adjps_ready = sem(main, "adjps_ready")
            adjT_ready = sem(main, "adjT_ready")
            x_in2 = sem(main, "x_in2")
            x_free2 = sem(main, "x_free2")
            uw_in = [sem(main, f"uw_in{i}") for i in range(2)]
            src_in = [sem(main, f"src_in{i}") for i in range(2)]
            mask_made = sem(main, "mask_made")
            mask_used = sem(main, "mask_used")
            masks_done = sem(main, "masks_done")
            gat_head = sem(main, "gat_head")
            wall_ready = sem(main, "wall_ready")
            gat_out = sem(main, "gat_out")
            chain0 = sem(main, "chain0")
            elu_min = sem(main, "elu_min")
            elu_exp = sem(main, "elu_exp")
            mid = sem(main, "mid")
            var_ready = sem(main, "var_ready")
            var_eps = sem(main, "var_eps")
            rstd_ready = sem(main, "rstd_ready")
            x1_ready = sem(main, "x1_ready")
            q_hi = sem(main, "q_hi")
            q_lo = sem(main, "q_lo")
            qn_ready = sem(main, "qn_ready")
            qn_all = sem(main, "qn_all")
            qk_ready = sem(main, "qk_ready")
            qk_root = sem(main, "qk_root")
            shift_ready = sem(main, "shift_ready")
            shh_ready = sem(main, "shh_ready")
            qps_ready = sem(main, "qps_ready")
            qT_ready = sem(main, "qT_ready")
            kT_in = [sem(main, f"kT_in{i}") for i in range(2)]
            v_in2 = [sem(main, f"v_in2{i}") for i in range(2)]
            s_ready = sem(main, "s_ready")
            s_free = sem(main, "s_free")
            e_ready = sem(main, "e_ready")
            phi_ready = sem(main, "phi_ready")
            phi_dve = sem(main, "phi_dve")
            plo_done = sem(main, "plo_done")
            pv_done = sem(main, "pv_done")
            att_head = sem(main, "att_head")
            att_out = sem(main, "att_out")
            chain1 = sem(main, "chain1")
            chain2 = sem(main, "chain2")
            fin = sem(main, "fin")
            pool_held2 = sem(main, "pool_held2")
            dve_held = sem(main, "dve_held")
            y_ready = sem(main, "y_ready")
            out_done = sem(main, "out_done")

            with nc.Block() as block:

                @block.sync
                def _(sp):
                    def load_adj(b, step):
                        sp.dma_start(adj_s[:], adj_b[bass.ds(b, 1), :, :, bass.ds(step * IB, IB)].rearrange("o p s j -> p (o s) j")).then_inc(adj_in, 16)

                    with sp.Fori(0, H) as st:
                        sp.wait_ge(adj_free, st + 1)
                        load_adj(0, st)
                    with sp.Fori(0, NB) as b:
                        sp.wait_ge(x_free2, b + 1)
                        sp.dma_start(X[:], x_b[bass.ds(b, 1)].rearrange("o p s d -> p (o s) d")).then_inc(x_in2, 16)
                        with sp.Fori(0, H // 2) as hp:
                            for i in range(2):
                                h = hp * 2 + i
                                sp.wait_ge(gat_head, b * H + h + 1)
                                sp.dma_start(uw[:, i], uw_d[bass.ds(h, 1)].rearrange("o p t c -> p (o t) c")).then_inc(uw_in[i], 16)
                                sp.dma_start(
                                    src_bc[:, i, :], src_d[bass.ds(h, 1), bass.ds(b * IB, IB)].rearrange("o n -> (o n)").partition_broadcast(P)
                                ).then_inc(src_in[i], 16)
                        nb = (b + 1) % NB
                        with sp.Fori(0, H // 2) as hp:
                            for i in range(2):
                                h = hp * 2 + i
                                sp.wait_ge(adj_free, (b + 1) * H + h + 1)
                                load_adj(nb, h)
                                sp.wait_ge(att_head, b * H + h + 1)
                                sp.dma_start(kT[:, i, :], kT_d[bass.ds(h, 1)].rearrange("o p n -> p (o n)")).then_inc(kT_in[i], 16)
                                sp.dma_start(vs[:, i], v_d[bass.ds(h, 1)].rearrange("o p t c -> p (o t) c")).then_inc(v_in2[i], 16)

                @block.gpsimd
                def _(pool):
                    def hold(semaphore, value):
                        pool.wait_ge(semaphore, value)
                        pool.sem_inc(pool_held2, 1)

                    nc.gpsimd.memset(mhalf[:], -0.5).then_inc(fin, 1)
                    nc.gpsimd.memset(phalf[:], 0.5).then_inc(fin, 1)
                    pool.sem_inc(adj_free, 1)
                    pool.sem_inc(x_free2, 1)

                    def convert(done):
                        hold(adj_in, done * 16 + 16)
                        hold(adjn_read, done + 1)
                        nc.gpsimd.tensor_scalar(adj_n[:], adj_s[:], 0.0, None, ALU.is_gt).then_inc(adjn_ready, 1)
                        hold(adjn_ready, done + 1)
                        pool.sem_inc(adj_free, 1)

                    def rstd_step(n):
                        hold(var_ready, n + 1)
                        nc.gpsimd.tensor_scalar(rstd[:], mv[:, :, 1], EPS, None, ALU.add).then_inc(var_eps, 1)
                        pool.wait_ge(var_eps, n + 1)
                        nc.gpsimd.tensor_tensor(rstd[:], rstd[:], mhalf[:], ALU.pow).then_inc(rstd_ready, 1)

                    pool.wait_ge(fin, 2)
                    with pool.Fori(0, H) as st:
                        convert(st)
                    with pool.Fori(0, NB) as b:
                        rstd_step(b * 2)
                        hold(qn_ready, b + 1)
                        nc.gpsimd.partition_all_reduce(qam[:], qm[:], P, RMAX).then_inc(qn_all, 1)
                        hold(qn_all, b + 1)
                        nc.gpsimd.tensor_tensor(qk2[:], qam[:], kmax2[:], ALU.mult).then_inc(qk_ready, 1)
                        hold(qk_ready, b + 1)
                        nc.gpsimd.tensor_tensor(qk2[:], qk2[:], phalf[:], ALU.pow).then_inc(qk_root, 1)
                        with pool.Fori(0, H) as st:
                            convert((b + 1) * H + st)
                        rstd_step(b * 2 + 1)

                @block.tensor
                def _(pe):
                    for s_, n_ in ((mask_used, RING), (gat_head, 2), (adjn_read, 1), (att_head, 2), (pv_done, 2)):
                        pe.sem_inc(s_, n_)

                    def adj_step(done):
                        pe.wait_ge(adjn_ready, done + 1)
                        for half in range(2):
                            adj_half(done, half)

                    def adj_half(done, half):
                        if half == 0:
                            pe.wait_ge(adjn_ready, done + 1)
                        pe.wait_ge(adjT_ready, done * 2 + half + 1)
                        for t in range(2):
                            for s in range(SUB):
                                last = nc.tensor.transpose(psA[:, t, s, :], adj_n[:, s, (half * 2 + t) * P : (half * 2 + t + 1) * P], identb[:])
                        last.then_inc(adjps_ready, 1)
                        if half == 1:
                            pe.wait_ge(adjps_ready, done * 2 + 2)
                            pe.sem_inc(adjn_read, 1)

                    def q_step(done, h):
                        pe.wait_ge(qT_ready, done + 1)
                        for kind in range(2):
                            for s in range(SUB):
                                last = nc.tensor.transpose(
                                    psQ[:, kind, s * P : (s + 1) * P],
                                    qq[:, s, bass.ds(h, 1), kind : kind + 2, :].rearrange("p o k f -> p (o k f)"),
                                    ident16[:],
                                )
                        last.then_inc(qps_ready, 1)

                    with pe.Fori(0, H) as st:
                        adj_step(st)
                    with pe.Fori(0, NB) as b:
                        with pe.Fori(0, H // 2) as hp:
                            for i in range(2):
                                hb = b * H + hp * 2 + i
                                pe.wait_ge(uw_in[i], (b * (H // 2) + hp) * 16 + 16)
                                pe.wait_ge(gat_out, hb + 1)
                                if i == 0:
                                    pe.wait_ge(wall_ready, hb + 1)
                                for jt in range(NT):
                                    pe.wait_ge(mask_made, hb * NT + jt + 1)
                                    for s in range(SUB):
                                        for half in range(2):
                                            last = nc.tensor.matmul(
                                                psU[i][:, s // 2, s % 2, :], mpos[:, jt % RING, s * P : (s + 1) * P],
                                                uw[:, i, jt, half * UW : (half + 1) * UW],
                                                start=(jt == 0 and s % 2 == 0 and half == 0), stop=(jt == NT - 1), skip_group_check=True,
                                            )
                                    last.then_inc(mask_used, 1)
                                    for s in range(SUB):
                                        for half in range(2):
                                            last = nc.tensor.matmul(
                                                psW[i][:, s, :], adjT[:, jt, s * P : (s + 1) * P],
                                                uw[:, i, jt, half * UW + F1 : half * UW + 2 * F1],
                                                start=(jt == 0 and s == 0 and half == 0), stop=(jt == NT - 1), skip_group_check=True,
                                            )
                                last.then_inc(gat_head, 1)
                        pe.wait_ge(q_lo, b + 1)
                        q_step(b * (H + 1), 0)
                        with pe.Fori(0, H // 2) as hp:
                            for i in range(2):
                                h = hp * 2 + i
                                hb = b * H + h
                                pe.wait_ge(kT_in[i], (b * (H // 2) + hp) * 16 + 16)
                                pe.wait_ge(v_in2[i], (b * (H // 2) + hp) * 16 + 16)
                                pe.wait_ge(qT_ready, b * (H + 1) + h + 2)
                                pe.wait_ge(att_out, hb + 1)

                                def scores(g):
                                    pe.wait_ge(s_free, hb * GROUPS + g + 1)
                                    for t in range(2):
                                        jt = 2 * g + t
                                        dst = psS[g % 2][:, t * IB : (t + 1) * IB]
                                        for kind in range(2):
                                            nc.tensor.matmul(dst, kT[:, i, jt * P : (jt + 1) * P], qT[:, i, kind, :], start=(kind == 0), stop=False)
                                        last = nc.tensor.matmul(dst, maskI[:], nmT[:, jt, :], start=False, stop=True)
                                    last.then_inc(s_ready, 1)

                                def weigh(g):
                                    pe.wait_ge(plo_done, hb * GROUPS + g + 1 + 2)
                                    for t in range(2):
                                        jt = 2 * g + t
                                        for s in range(SUB):
                                            at = slice(t * IB + s * P, t * IB + (s + 1) * P)
                                            for w, half in ((phi, 0), (phi, 1), (plo, 0)):
                                                last = nc.tensor.matmul(
                                                    psO[i][:, s, :], w[:, g % 2, at], vs[:, i, jt, half * F1 : (half + 1) * F1],
                                                    start=(jt == 0 and s == 0 and w is phi and half == 0), stop=(jt == NT - 1), skip_group_check=True,
                                                )
                                    last.then_inc(pv_done, 1)

                                scores(0)
                                scores(1)
                                for g in range(GROUPS):
                                    if g + 2 < GROUPS:
                                        scores(g + 2)
                                    weigh(g)
                                    if g == 4:
                                        adj_half((b + 1) * H + h, 0)
                                    if g == 8:
                                        adj_half((b + 1) * H + h, 1)
                                    if g == 10:
                                        q_step(b * (H + 1) + h + 1, (h + 1) % H)
                                pe.wait_ge(pv_done, hb * GROUPS + GROUPS + 2)
                                pe.sem_inc(att_head, 1)

                @block.scalar
                def _(act):
                    for s_, n_ in ((wall_ready, 1), (s_free, 2), (qT_ready, 1)):
                        act.sem_inc(s_, n_)

                    def q_copy(done, i):
                        act.wait_ge(qps_ready, done + 1)
                        act.activation(qT[:, i], psQ[:], ACT.Copy).then_inc(qT_ready, 1)

                    with act.Fori(0, NB) as b:
                        with act.Fori(0, H // 2) as hp:
                            for i in range(2):
                                hb = b * H + hp * 2 + i
                                act.wait_ge(gat_head, hb + 1 + 2)
                                act.wait_ge(gat_out, hb + 1)
                                act.activation(wall[:, i], psW[i], ACT.Copy).then_inc(wall_ready, 1)
                        act.wait_ge(elu_min, b + 1)
                        act.activation(Ef, Ef, ACT.Exp).then_inc(elu_exp, 1)
                        act.wait_ge(x1_ready, b + 1)
                        for k in (0, 2):
                            act.activation(qq[:, :, :, k, :], X[:].rearrange("p s (h f) -> p s h f", h=H), ACT.Copy, scale=SCALE).then_inc(q_hi, 1)
                        q_copy(b * (H + 1), 0)
                        act.wait_ge(shift_ready, b + 1)
                        with act.Fori(0, H // 2) as hp:
                            for i in range(2):
                                h = hp * 2 + i
                                hb = b * H + h
                                act.wait_ge(att_head, hb + 1)
                                act.activation(shift_h[:, i, :], shift[:, bass.ds(h, 1)], ACT.Copy).then_inc(shh_ready, 1)
                                act.wait_ge(shh_ready, hb + 1)
                                for g in range(GROUPS):
                                    n = hb * GROUPS + g
                                    act.wait_ge(s_ready, n + 1)
                                    act.wait_ge(plo_done, n + 1)
                                    e = act.activation(E[:, g % 2, :], psS[g % 2], ACT.Exp, bias=shift_h[:, i, :])
                                    e.then_inc(e_ready, 1)
                                    if g % 2 == 1:
                                        act.wait_ge(pv_done, n + 1)
                                        act.activation(phi[:, 1, :], psS[1], ACT.Exp, bias=shift_h[:, i, :]).then_inc(phi_ready, 1)
                                        act.wait_ge(phi_ready, hb * (GROUPS // 2) + g // 2 + 1)
                                    else:
                                        act.wait_ge(e_ready, n + 1)
                                    act.sem_inc(s_free, 1)
                                    if g == 12:
                                        q_copy(b * (H + 1) + h + 1, 1 - i)
                        act.wait_ge(y_ready, b + 1)
                        act.dma_start(out_b[bass.ds(b, 1)].rearrange("o p s d -> p (o s) d"), O[:]).then_inc(out_done, 16)
                    act.wait_ge(out_done, 16 * NB + 16)

                @block.vector
                def _(dve):
                    for s_, n_ in ((adjT_ready, 1), (gat_out, 2), (att_out, 2), (plo_done, 2), (out_done, 16)):
                        dve.sem_inc(s_, n_)

                    def adj_copy(done, half, st):
                        dve.wait_ge(adjps_ready, done * 2 + half + 1)
                        nc.vector.tensor_copy(
                            adjT[:, bass.ds(st * 4 + half * 2, 2), :].rearrange("p t n -> p (t n)"), psA.rearrange("p t s n -> p (t s n)")
                        ).then_inc(adjT_ready, 1)

                    def gat_finish(b, h, i):
                        hb = b * H + h
                        dve.wait_ge(wall_ready, hb + 1 + 1)
                        a_pos = fac[:, 0, :, bass.ds(h, 1)].to_broadcast([P, SUB, F1])
                        a_neg = fac[:, 1, :, bass.ds(h, 1)].to_broadcast([P, SUB, F1])
                        for bank in range(2):
                            rows = slice(2 * bank, 2 * bank + 2)
                            nc.vector.tensor_tensor(t1_[:, rows, :], wall[:, i, rows, :], psU[i][:, bank, :, F1:UW], ALU.subtract).then_inc(chain0, 1)
                            nc.vector.tensor_tensor(t2_[:, rows, :], psU[i][:, bank, :, 0:F1], a_pos[:, rows, :], ALU.mult).then_inc(chain0, 1)
                        dve.wait_ge(chain0, hb * 8 + 4)
                        nc.vector.tensor_tensor(t1_[:], t1_[:], a_neg, ALU.mult).then_inc(chain0, 1)
                        dve.wait_ge(chain0, hb * 8 + 5)
                        nc.vector.tensor_tensor(t1_[:], t1_[:], t2_[:], ALU.add).then_inc(chain0, 1)
                        dve.wait_ge(chain0, hb * 8 + 6)
                        nc.vector.reciprocal(rden[:], t1_[:, :, F]).then_inc(chain0, 1)
                        dve.wait_ge(chain0, hb * 8 + 7)
                        nc.vector.tensor_tensor(
                            O[:, :, bass.ds(h * F, F)], t1_[:, :, 0:F], rden[:].unsqueeze(2).to_broadcast([P, SUB, F]), ALU.mult
                        ).then_inc(chain0, 1)
                        dve.wait_ge(chain0, hb * 8 + 8)
                        dve.sem_inc(gat_out, 1)

                    def att_finish(b, h, i):
                        hb = b * H + h
                        dve.wait_ge(att_head, hb + 1 + 2)
                        nc.vector.reciprocal(rden[:], psO[i][:, :, F]).then_inc(chain1, 1)
                        dve.wait_ge(chain1, hb * 2 + 1)
                        nc.vector.tensor_tensor(
                            O[:, :, bass.ds(h * F, F)], psO[i][:, :, 0:F], rden[:].unsqueeze(2).to_broadcast([P, SUB, F]), ALU.mult
                        ).then_inc(chain1, 1)
                        dve.wait_ge(chain1, hb * 2 + 2)
                        dve.sem_inc(att_out, 1)

                    def gat_head_masks(b, h, i, pair, finish_before):
                        hb = b * H + h
                        nc.vector.tensor_copy(dst_h[:, i, :], neg_dst[:, :, bass.ds(h, 1)].rearrange("p t o -> p (t o)")).then_inc(masks_done, 1)
                        dve.wait_ge(masks_done, hb + 1)
                        dve.wait_ge(src_in[i], (b * (H // 2) + pair) * 16 + 16)
                        for jt in range(NT):
                            if jt == 8 and finish_before:
                                gat_finish(b, h - 1, 1 - i)
                            dve.wait_ge(mask_used, hb * NT + jt + 1)
                            nc.vector.scalar_tensor_tensor(
                                mpos[:, jt % RING, :], src_bc[:, i, :], dst_h[:, i, jt : jt + 1], adjT[:, jt, :], ALU.is_gt, ALU.mult
                            ).then_inc(mask_made, 1)

                    def att_groups(b, h, i, finish_before):
                        hb = b * H + h
                        for g in range(GROUPS):
                            n = hb * GROUPS + g
                            if g == 3 and finish_before:
                                att_finish(b, h - 1, 1 - i)
                            dve.wait_ge(e_ready, n + 1)
                            if g % 2 == 0:
                                dve.wait_ge(pv_done, n + 1)
                                nc.vector.tensor_copy(phi[:, 0, :], E[:, 0, :]).then_inc(phi_dve, 1)
                                dve.wait_ge(phi_dve, hb * (GROUPS // 2) + g // 2 + 1)
                            else:
                                dve.wait_ge(phi_ready, hb * (GROUPS // 2) + g // 2 + 1)
                            nc.vector.tensor_tensor(plo[:, g % 2, :], E[:, g % 2, :], phi[:, g % 2, :], ALU.subtract).then_inc(plo_done, 1)
                            if g == 5:
                                adj_copy((b + 1) * H + h, 0, h)
                            if g == 9:
                                adj_copy((b + 1) * H + h, 1, h)

                    with dve.Fori(0, H) as st:
                        for half in range(2):
                            adj_copy(st, half, st)
                    with dve.Fori(0, NB) as b:
                        for k, w in ((0, pos_w), (1, neg_w)):
                            nc.vector.tensor_copy(fac[:, k], w[:, bass.ds(b * SUB, SUB), :]).then_inc(mid, 1)
                        dve.wait_ge(out_done, b * 16 + 16)
                        dve.wait_ge(adjT_ready, (b + 1) * 2 * H + 1)
                        gat_head_masks(b, 0, 0, 0, False)
                        with dve.Fori(0, H // 2 - 1) as hp:
                            gat_head_masks(b, hp * 2 + 1, 1, hp, True)
                            gat_head_masks(b, hp * 2 + 2, 0, hp + 1, True)
                        gat_head_masks(b, H - 1, 1, H // 2 - 1, True)
                        nc.vector.tensor_scalar(
                            nmT[:].rearrange("p t n -> p (t n)"), adjT[:].rearrange("p t n -> p (t n)"), -1.0, 1.0, ALU.mult, ALU.add
                        ).then_inc(mid, 1)
                        gat_finish(b, H - 1, 1)
                        nc.vector.tensor_scalar(Ef, Of, 0.0, None, ALU.min).then_inc(elu_min, 1)
                        dve.wait_ge(elu_exp, b + 1)
                        nc.vector.scalar_tensor_tensor(Of, Of, 0.0, Ef, ALU.max, ALU.add).then_inc(mid, 1)
                        dve.wait_ge(mid, b * 16 + 4)
                        dve.wait_ge(x_in2, b * 16 + 16)
                        nc.vector.scalar_tensor_tensor(Xf, Of, -1.0, Xf, ALU.add, ALU.add).then_inc(mid, 1)
                        dve.wait_ge(mid, b * 16 + 5)
                        for s in range(SUB):
                            nc.vector.bn_stats(stats[:, s, :], X[:, s, :]).then_inc(mid, 1)
                        dve.wait_ge(mid, b * 16 + 9)
                        dve.sem_inc(dve_held, 1)
                        for s in range(SUB):
                            last = nc.vector.bn_aggr(mv[:, s, :], stats[:, s, :]).then_inc(mid, 1)
                        dve.wait_ge(mid, b * 16 + 13)
                        dve.sem_inc(var_ready, 1)
                        dve.wait_ge(rstd_ready, b * 2 + 1)
                        for s in range(SUB):
                            last = nc.vector.tensor_scalar(X[:, s, :], X[:, s, :], mv[:, s, 0:1], rstd[:, s : s + 1], ALU.subtract, ALU.mult)
                            if s < SUB - 1:
                                continue
                            last.then_inc(x1_ready, 1)
                        dve.wait_ge(x1_ready, b + 1)
                        nc.vector.tensor_tensor(Ef, Xf, Xf, ALU.mult).then_inc(mid, 1)
                        dve.wait_ge(mid, b * 16 + 14)
                        nc.vector.tensor_reduce(
                            qn2[:].rearrange("p s h -> p (s h)"), Ef.rearrange("p (n f) -> p n f", f=F), AX_X, ALU.add
                        ).then_inc(mid, 1)
                        dve.wait_ge(mid, b * 16 + 15)
                        nc.vector.tensor_reduce(qm[:], qn2[:].rearrange("p s h -> p h s"), AX_X, ALU.max).then_inc(qn_ready, 1)
                        dve.wait_ge(q_hi, b * 2 + 2)
                        for s in range(SUB):
                            last = nc.vector.scalar_tensor_tensor(
                                qq[:, s, :, 1, :], X[:, s, :].rearrange("p (h f) -> p h f", h=H), SCALE, qq[:, s, :, 0, :], ALU.mult, ALU.subtract
                            )
                        last.then_inc(q_lo, 1)
                        dve.wait_ge(qk_root, b + 1)
                        nc.vector.tensor_scalar(shift[:], qk2[:], -SCALE * 1.0001, LOG_ATT_SCALE, ALU.mult, ALU.add).then_inc(shift_ready, 1)
                        att_groups(b, 0, 0, False)
                        with dve.Fori(0, H // 2 - 1) as hp:
                            att_groups(b, hp * 2 + 1, 1, True)
                            att_groups(b, hp * 2 + 2, 0, True)
                        att_groups(b, H - 1, 1, True)
                        att_finish(b, H - 1, 1)
                        nc.vector.tensor_tensor(Of, Of, Xf, ALU.add).then_inc(mid, 1)
                        dve.wait_ge(mid, b * 16 + 16)
                        dve.sem_inc(x_free2, 1)
                        for s in range(SUB):
                            nc.vector.bn_stats(stats[:, s, :], O[:, s, :]).then_inc(chain2, 1)
                        dve.wait_ge(chain2, b * 8 + 4)
                        dve.sem_inc(dve_held, 1)
                        for s in range(SUB):
                            nc.vector.bn_aggr(mv[:, s, :], stats[:, s, :]).then_inc(chain2, 1)
                        dve.wait_ge(chain2, b * 8 + 8)
                        dve.sem_inc(var_ready, 1)
                        dve.wait_ge(rstd_ready, b * 2 + 2)
                        for s in range(SUB):
                            last = nc.vector.tensor_scalar(O[:, s, :], O[:, s, :], mv[:, s, 0:1], rstd[:, s : s + 1], ALU.subtract, ALU.mult)
                        last.then_inc(y_ready, 1)


_INS = ["x", "adj", "L0_gnn_W", "L0_gnn_a", "L1_gnn_x2", "L1_gnn_v"]


def kernel(**inputs):
    import numpy as _np
    import concourse.bacc as _bacc
    from concourse import mybir as _mybir
    from concourse.bass_utils import run_bass_kernel_spmd as _run

    nc = _bacc.Bacc("TRN2", target_bir_lowering=False, num_devices=1)
    arrays, args = {}, []
    for name in _INS:
        arr = _np.ascontiguousarray(inputs[name])
        arrays[f"in_{name}_dram"] = arr
        args.append(nc.dram_tensor(f"in_{name}_dram", arr.shape, _mybir.dt.from_np(arr.dtype), kind="ExternalInput").ap())
    shape = tuple(arrays["in_x_dram"].shape)
    args.append(nc.dram_tensor("out_0_dram", shape, _mybir.dt.float32, kind="ExternalOutput").ap())
    bass_gat_then_masked_attention(nc, *args)
    r = _run(nc, [arrays], core_ids=[0])
    return r.results[0]["out_0_dram"]
```

```python
from contextlib import ExitStack

import numpy as np

import concourse.bass as bass
from concourse import mybir

P = 128
ALU = mybir.AluOpType
ACT = mybir.ActivationFunctionType
F32 = mybir.dt.float32
F16 = mybir.dt.float16
BF16 = mybir.dt.bfloat16
I32 = mybir.dt.int32
AX_X = mybir.AxisListType.X
RMAX = bass.bass_isa.ReduceOp.max

SLOPE = 0.2
EPS = 1e-5
LOG_GAT_SCALE = float(10 * np.log(2.0))
LOG_ATT_SCALE = float(15 * np.log(2.0))
MASKED = -float(2.0**100)
W_UP = 256.0
STEP_UP = float(2.0**40)
LOG_W_UP = float(8 * np.log(2.0))
HALVES = ((0, 0), (1, 0), (0, 1))


def bass_gat_then_masked_attention(
    nc: bass.Bass,
    x: bass.AP,
    adj: bass.AP,
    W: bass.AP,
    a: bass.AP,
    x2: bass.AP,
    v: bass.AP,
    out: bass.AP,
):
    N, D = x.shape
    H, _, F = W.shape
    C = D // P
    NT = N // P
    SUB = 4
    IB = SUB * P
    NB = N // IB
    G = 4
    F1 = F + 1
    UW = 2 * F1
    PAIRS = NT // 2
    SPLIT = PAIRS // 2
    DIRECT = PAIRS - 2
    RING = 4
    GROUPS = NT // 2
    SCALE = float(F) ** -0.5
    assert D == H * F and F == 64 and N % IB == 0 and H % 2 == 0 and NT == 32

    uw_d = nc.dram_tensor("uw_scratch", (H, P, NT, 2 * UW), F16, kind="Internal").ap()
    kT_d = nc.dram_tensor("kT_scratch", (H, P, N), F16, kind="Internal").ap()
    v_d = nc.dram_tensor("v_scratch", (H, P, NT, 2 * F1), F16, kind="Internal").ap()
    src_d = nc.dram_tensor("src_scratch", (H, N), F32, kind="Internal").ap()

    x_t = x.rearrange("(t p) d -> t p d", p=P)
    x2_t = x2.rearrange("(t p) d -> t p d", p=P)
    v_t = v.rearrange("(t p) d -> t p d", p=P)
    x_b = x.rearrange("(b s p) d -> b p s d", s=SUB, p=P)
    out_b = out.rearrange("(b s p) d -> b p s d", s=SUB, p=P)
    adj_b = adj.rearrange("(b s p) j -> b p s j", s=SUB, p=P)

    with ExitStack() as whole:

        def sb(stack, name, shape, dt):
            return stack.enter_context(nc.sbuf_tensor(name, shape, dt))

        def ps(stack, name, shape, dt):
            return stack.enter_context(nc.psum_tensor(name, shape, dt))

        def sem(stack, name):
            return stack.enter_context(nc.semaphore(name))

        ident = sb(whole, "ident", [P, P], F32)
        ident16 = sb(whole, "ident16", [P, P], F16)
        identb = sb(whole, "identb", [P, P], BF16)
        maskI = sb(whole, "maskI", [P, P], BF16)
        dst_up = sb(whole, "dst_up", [P, NT, H], F32)
        pos_w = sb(whole, "pos_w", [P, NT, H], F32)
        neg_w = sb(whole, "neg_w", [P, NT, H], F32)
        kmax2 = sb(whole, "kmax2", [P, H], F32)
        adjT = sb(whole, "adjT", [P, NT, IB], BF16)

        with ExitStack() as prep:
            Wsb = sb(prep, "Wsb", [P, C, D], F32)
            abc = sb(prep, "abc", [P, H, 2, F], F32)
            wprod = sb(prep, "wprod", [P, H, F], F32)
            Wa = sb(prep, "Wa", [P, C, 2, H], F32)
            Wh = sb(prep, "Wh", [P, 2, C, D], F16)
            Wah = sb(prep, "Wah", [P, 2, C, 2 * H], F16)
            xT = sb(prep, "xT", [P, 2, C, N], F16)
            loads = sb(prep, "loads", [P, 2 * G * D], F32)
            x_s = loads[:, 0 : G * D].rearrange("p (k d) -> p k d", k=G)
            k_s = loads[:, G * D :].rearrange("p (k d) -> p k d", k=G)
            tw = loads[:, 0 : 4 * H * F1].rearrange("p (i h k f) -> p i h k f", i=2, h=H, k=2)
            v_s = sb(prep, "v_s", [P, G, D], F32)
            adj_i = v_s[:].bitcast(I32)
            adj_f = sb(prep, "adj_f", [P, SUB, IB], BF16)
            kk = sb(prep, "kk", [P, 2, H, 2, F], F16)
            kT_s = sb(prep, "kT_s", [P, 2, H, 2 * P], F16)
            vv = sb(prep, "vv", [P, 2, H, 2, 2 * F1], F16)
            ksq = sb(prep, "ksq", [P, D], F32)
            kn2 = sb(prep, "kn2", [P, NT, H], F32)
            fT = sb(prep, "fT", [2 * H, N], F32)
            fall = sb(prep, "fall", [P, NT, 2, H], F32)
            mx = sb(prep, "mx", [P, 2, H], F32)
            amx = sb(prep, "amx", [P, 2, H], F32)
            zz = sb(prep, "zz", [P, NT, H], F32)
            mm = sb(prep, "mm", [P, NT, H], F32)
            dd = sb(prep, "dd", [P, NT, H], F32)
            ee = sb(prep, "ee", [P, NT, H, 2], F32)
            lgs = sb(prep, "lgs", [P, 1], F32)
            uws = sb(prep, "uws", [P, 2, H, 2 * UW], F16)

            psT = [ps(prep, f"psT{i}", [P, 512], F32) for i in range(2)]
            psK = [ps(prep, f"psK{i}", [P, H, P], F16) for i in range(2)]
            psF = ps(prep, "psF", [P, 512], F32)
            psD = ps(prep, "psD", [P, NT, 2 * H], F32)
            psH = psT
            psM = ps(prep, "psM", [P, 2, SUB, P], BF16)

            w_in = sem(prep, "w_in")
            ids = sem(prep, "ids")
            wa_chain = sem(prep, "wa_chain")
            x_in = [sem(prep, f"x_in{i}") for i in range(G)]
            k_in = [sem(prep, f"k_in{i}") for i in range(G)]
            v_in = [sem(prep, f"v_in{i}") for i in range(G)]
            x_used = sem(prep, "x_used")
            k_used = sem(prep, "k_used")
            v_used = sem(prep, "v_used")
            xT_ps = sem(prep, "xT_ps")
            xT_hi = sem(prep, "xT_hi")
            xT_sb = sem(prep, "xT_sb")
            w_hi = sem(prep, "w_hi")
            w_lo = sem(prep, "w_lo")
            fT_ps = sem(prep, "fT_ps")
            fT_sb = sem(prep, "fT_sb")
            khi = sem(prep, "khi")
            klo = sem(prep, "klo")
            ksq_done = sem(prep, "ksq_done")
            kn_done = sem(prep, "kn_done")
            kT_ps = sem(prep, "kT_ps")
            kT_sb = sem(prep, "kT_sb")
            kT_out = [sem(prep, f"kT_out{i}") for i in range(2)]
            vhi = sem(prep, "vhi")
            vlo = sem(prep, "vlo")
            v_ones = sem(prep, "v_ones")
            vv_out = [sem(prep, f"vv_out{i}") for i in range(2)]
            d_ps = sem(prep, "d_ps")
            d_sb = sem(prep, "d_sb")
            fmax = sem(prep, "fmax")
            amax = sem(prep, "amax")
            src_out = sem(prep, "src_out")
            ph = sem(prep, "ph")
            ph_act = sem(prep, "ph_act")
            hp_ps = sem(prep, "hp_ps")
            hp_used = sem(prep, "hp_used")
            t_made = sem(prep, "t_made")
            uw_hi = sem(prep, "uw_hi")
            uw_lo = sem(prep, "uw_lo")
            uw_out = [sem(prep, f"uw_out{i}") for i in range(2)]
            m_in = sem(prep, "m_in")
            m_conv = sem(prep, "m_conv")
            m_used = sem(prep, "m_used")
            m_ps = sem(prep, "m_ps")
            m_sb = sem(prep, "m_sb")
            pool_held = sem(prep, "pool_held")

            with nc.Block() as block:

                @block.sync
                def _(sp):
                    for c in range(C):
                        sp.dma_start(
                            Wsb[:, c, :].rearrange("p (h f) -> p h f", h=H),
                            W[:, c * P : (c + 1) * P, :].rearrange("h p f -> p h f"),
                        ).then_inc(w_in, 16)
                    sp.dma_start(
                        abc[:].rearrange("p h k f -> p (h k f)"),
                        a.rearrange("h f -> (h f)").partition_broadcast(P),
                    ).then_inc(w_in, 16)
                    with sp.Fori(0, NT // G) as g:
                        for k in range(G):
                            sp.wait_ge(x_used, g * G + k + 1)
                            sp.dma_start(x_s[:, k, :], x_t[bass.ds(g * G + k, 1)].rearrange("o p d -> p (o d)")).then_inc(x_in[k], 16)
                            sp.wait_ge(k_used, g * G + k + 1)
                            sp.dma_start(k_s[:, k, :], x2_t[bass.ds(g * G + k, 1)].rearrange("o p d -> p (o d)")).then_inc(k_in[k], 16)
                            sp.wait_ge(v_used, g * G + k + 1)
                            sp.dma_start(v_s[:, k, :], v_t[bass.ds(g * G + k, 1)].rearrange("o p d -> p (o d)")).then_inc(v_in[k], 16)
                    sp.wait_ge(v_used, NT + G)
                    with sp.Fori(0, H) as st:
                        sp.wait_ge(m_conv, st + 1)
                        sp.dma_start(adj_i, adj_b[0:1, :, :, bass.ds(st * IB, IB)].rearrange("o p s j -> p (o s) j")).then_inc(m_in, 16)

                @block.gpsimd
                def _(pool):
                    def hold(semaphore, value):
                        pool.wait_ge(semaphore, value)
                        pool.sem_inc(pool_held, 1)

                    nc.gpsimd.memset(ident[:], 0.0).then_inc(ids, 1)
                    nc.gpsimd.memset(vv[:], 0.0).then_inc(v_ones, 1)
                    pool.wait_ge(v_ones, 1)
                    nc.gpsimd.memset(vv[:, :, :, :, F : F + 1], 1.0).then_inc(v_ones, 1)
                    pool.wait_ge(ids, 1)
                    nc.gpsimd.affine_select(
                        out=ident[:], in_=ident[:], compare_op=ALU.not_equal, fill=1.0, base=0,
                        pattern=[[-1, P]], channel_multiplier=1,
                    ).then_inc(ids, 1)
                    pool.wait_ge(ids, 2)
                    nc.gpsimd.tensor_copy(ident16[:], ident[:]).then_inc(ids, 1)
                    nc.gpsimd.tensor_copy(identb[:], ident[:]).then_inc(ids, 1)
                    nc.gpsimd.tensor_scalar(maskI[:], ident[:], MASKED, None, ALU.mult).then_inc(ids, 1)
                    pool.sem_inc(v_used, G)
                    pool.sem_inc(vlo, 2)
                    pool.sem_inc(m_conv, 1)
                    pool.wait_ge(v_ones, 2)
                    with pool.Fori(0, NT // G) as g:
                        for k in range(G):
                            i, half = k // 2, k % 2
                            src = v_s[:, k, :].rearrange("p (h f) -> p h f", h=H)
                            hold(v_in[k], g * 16 + 16)
                            if half == 0:
                                hold(vv_out[i], g * 16)
                            nc.gpsimd.tensor_copy(vv[:, i, :, half, 0:F], src).then_inc(vhi, 1)
                            pool.wait_ge(vhi, g * G + k + 1)
                            nc.gpsimd.tensor_tensor(
                                vv[:, i, :, half, F1 : F1 + F], src, vv[:, i, :, half, 0:F], ALU.subtract
                            ).then_inc(vlo, 1)
                            hold(vlo, g * G + k + 3)
                            pool.sem_inc(v_used, 1)
                            if half == 1:
                                pool.dma_start(
                                    v_d[:, :, bass.ds((g * 2 + i) * 2, 2), :].rearrange("h p t c -> p h t c"), vv[:, i]
                                ).then_inc(vv_out[i], 16)
                    pool.wait_ge(fmax, 2)
                    nc.gpsimd.partition_all_reduce(
                        amx[:].rearrange("p k h -> p (k h)"), mx[:].rearrange("p k h -> p (k h)"), P, RMAX
                    ).then_inc(amax, 1)
                    with pool.Fori(0, H) as st:
                        hold(m_in, st * 16 + 16)
                        hold(m_used, st + 1)
                        nc.gpsimd.tensor_scalar(adj_f[:], adj_i, 0.0, None, ALU.is_gt).then_inc(m_conv, 1)
                    for i in range(2):
                        pool.wait_ge(vv_out[i], 16 * (NT // G))

                @block.vector
                def _(dve):
                    for s_, n_ in ((k_used, G), (klo, 2), (xT_sb, 2), (fT_sb, 1), (hp_used, 2), (uw_lo, 2), (m_sb, 1)):
                        dve.sem_inc(s_, n_)
                    nc.vector.memset(lgs[:], LOG_GAT_SCALE - LOG_W_UP).then_inc(ph, 1)
                    dve.wait_ge(w_in, 16 * (C + 1))
                    n = 0
                    for c in range(C):
                        for k in range(2):
                            nc.vector.tensor_tensor(
                                wprod[:], Wsb[:, c, :].rearrange("p (h f) -> p h f", h=H), abc[:, :, k, :], ALU.mult
                            ).then_inc(wa_chain, 1)
                            n += 1
                            dve.wait_ge(wa_chain, n)
                            nc.vector.tensor_reduce(Wa[:, c, k, :], wprod[:], AX_X, ALU.add).then_inc(wa_chain, 1)
                            n += 1
                            dve.wait_ge(wa_chain, n)
                    dve.wait_ge(w_hi, 2)
                    nc.vector.scalar_tensor_tensor(
                        Wh[:, 1].rearrange("p c d -> p (c d)"), Wsb[:].rearrange("p c d -> p (c d)"), W_UP,
                        Wh[:, 0].rearrange("p c d -> p (c d)"), ALU.mult, ALU.subtract,
                    ).then_inc(w_lo, 1)
                    nc.vector.scalar_tensor_tensor(
                        Wah[:, 1].rearrange("p c n -> p (c n)"), Wa[:].rearrange("p c k h -> p (c k h)"), W_UP,
                        Wah[:, 0].rearrange("p c n -> p (c n)"), ALU.mult, ALU.subtract,
                    ).then_inc(w_lo, 1)
                    with dve.Fori(0, NT // G) as g:
                        for k in range(G):
                            i = k % 2
                            t1 = g * G + k + 1
                            dve.wait_ge(khi, t1)
                            nc.vector.tensor_tensor(
                                kk[:, i, :, 1, :], k_s[:, k, :].rearrange("p (h f) -> p h f", h=H), kk[:, i, :, 0, :], ALU.subtract
                            ).then_inc(klo, 1)
                            nc.vector.tensor_tensor(ksq[:], k_s[:, k, :], k_s[:, k, :], ALU.mult).then_inc(ksq_done, 1)
                            dve.wait_ge(ksq_done, t1)
                            dve.sem_inc(k_used, 1)
                            nc.vector.tensor_reduce(
                                kn2[:, bass.ds(g * G + k, 1), :].rearrange("p o h -> p (o h)"),
                                ksq[:].rearrange("p (h f) -> p h f", h=H), AX_X, ALU.add,
                            ).then_inc(kn_done, 1)
                            dve.wait_ge(xT_hi, t1)
                            nc.vector.tensor_tensor(
                                xT[:, 1, :, bass.ds((g * G + k) * P, P)], psT[i][:].rearrange("p (c n) -> p c n", c=C),
                                xT[:, 0, :, bass.ds((g * G + k) * P, P)], ALU.subtract,
                            ).then_inc(xT_sb, 1)
                            dve.wait_ge(kn_done, t1)
                        dve.wait_ge(fT_ps, g + 1)
                        nc.vector.tensor_scalar(fT[:, bass.ds(g * 512, 512)], psF[0 : 2 * H, :], 1.0 / W_UP, None, ALU.mult).then_inc(fT_sb, 1)
                    dve.wait_ge(d_ps, 1)
                    nc.vector.tensor_copy(fall[:].rearrange("p t k h -> p t (k h)"), psD[:]).then_inc(d_sb, 1)
                    dve.wait_ge(d_sb, 1)
                    nc.vector.tensor_reduce(mx[:, 0, :], fall[:, :, 1, :].rearrange("p t h -> p h t"), AX_X, ALU.max).then_inc(fmax, 1)
                    nc.vector.tensor_reduce(mx[:, 1, :], kn2[:].rearrange("p t h -> p h t"), AX_X, ALU.max).then_inc(fmax, 1)
                    nc.vector.tensor_scalar(dst_up[:], fall[:, :, 1, :], STEP_UP, None, ALU.mult).then_inc(ph, 1)
                    dve.wait_ge(amax, 1)
                    top = amx[:, 0:1, :].to_broadcast([P, NT, H])
                    nc.vector.tensor_tensor(dd[:], fall[:, :, 1, :], top, ALU.subtract).then_inc(ph, 1)
                    nc.vector.tensor_tensor(zz[:], fall[:, :, 0, :], top, ALU.add).then_inc(ph, 1)
                    nc.vector.tensor_copy(kmax2[:], amx[:, 1, :]).then_inc(ph, 1)
                    dve.wait_ge(ph, 5)
                    nc.vector.scalar_tensor_tensor(mm[:], zz[:], SLOPE, zz[:], ALU.mult, ALU.max).then_inc(ph, 1)
                    dve.wait_ge(ph, 6)
                    nc.vector.tensor_tensor(pos_w[:], zz[:], mm[:], ALU.subtract).then_inc(ph, 1)
                    nc.vector.scalar_tensor_tensor(neg_w[:], zz[:], SLOPE, mm[:], ALU.mult, ALU.subtract).then_inc(ph, 1)
                    dve.wait_ge(ph_act, 2)
                    with dve.Fori(0, NT // G) as g:
                        for k in range(G):
                            i = k % 2
                            t1 = g * G + k + 1
                            dve.wait_ge(hp_ps, t1)
                            for kind in range(2):
                                nc.vector.tensor_tensor(
                                    tw[:, i, :, kind, 0:F],
                                    psH[i][:].rearrange("p (h f) -> p h f", h=H),
                                    ee[:, bass.ds(g * G + k, 1), :, kind : kind + 1].rearrange("p o h k -> p (o h) k").to_broadcast([P, H, F]),
                                    ALU.mult,
                                ).then_inc(t_made, 1)
                            nc.vector.tensor_scalar(
                                tw[:, i, :, :, F : F + 1].rearrange("p h k o -> p h (k o)"),
                                ee[:, bass.ds(g * G + k, 1), :, :].rearrange("p o h k -> p (o h) k"), W_UP, None, ALU.mult,
                            ).then_inc(t_made, 1)
                            dve.wait_ge(t_made, (g * G + k) * 3 + 3)
                            dve.sem_inc(hp_used, 1)
                            if k % 2 == 1:
                                half = k // 2
                                dve.wait_ge(m_ps, g * 2 + half + 1)
                                nc.vector.tensor_copy(
                                    adjT[:, bass.ds(g * 4 + half * 2, 2), :].rearrange("p t n -> p (t n)"), psM[:].rearrange("p t s n -> p (t s n)")
                                ).then_inc(m_sb, 1)
                            dve.wait_ge(uw_hi, t1)
                            nc.vector.tensor_tensor(
                                uws[:, i, :, UW : 2 * UW], tw[:, i].rearrange("p h k f -> p h (k f)"), uws[:, i, :, 0:UW], ALU.subtract
                            ).then_inc(uw_lo, 1)

                @block.scalar
                def _(act):
                    act.sem_inc(kT_sb, 2)
                    for i in range(2):
                        act.sem_inc(kT_out[i], 16)
                        act.sem_inc(uw_out[i], 16)
                    act.wait_ge(wa_chain, 4 * C)
                    act.activation(Wah[:, 0], Wa[:].rearrange("p c k h -> p c (k h)"), ACT.Copy, scale=W_UP).then_inc(w_hi, 1)
                    act.activation(Wh[:, 0], Wsb[:], ACT.Copy, scale=W_UP).then_inc(w_hi, 1)
                    with act.Fori(0, NT // G) as g:
                        for k in range(G):
                            i = k % 2
                            t1 = g * G + k + 1
                            act.wait_ge(k_in[k], g * 16 + 16)
                            act.wait_ge(kT_ps, t1)
                            act.activation(kk[:, i, :, 0, :], k_s[:, k, :].rearrange("p (h f) -> p h f", h=H), ACT.Copy).then_inc(khi, 1)
                            act.wait_ge(xT_ps, t1)
                            act.activation(
                                xT[:, 0, :, bass.ds((g * G + k) * P, P)], psT[i][:].rearrange("p (c n) -> p c n", c=C), ACT.Copy
                            ).then_inc(xT_hi, 1)
                            act.wait_ge(kT_ps, t1 + 2)
                            if i == 0:
                                act.wait_ge(kT_out[k // 2], g * 16 + 16)
                            act.activation(kT_s[:, k // 2, :, i * P : (i + 1) * P], psK[i][:], ACT.Copy).then_inc(kT_sb, 1)
                            if i == 1:
                                act.wait_ge(kT_sb, t1 + 2)
                                act.dma_start(
                                    kT_d[:, :, bass.ds((g * 2 + k // 2) * 2 * P, 2 * P)].rearrange("h p n -> p h n"), kT_s[:, k // 2]
                                ).then_inc(kT_out[k // 2], 16)
                    act.wait_ge(fT_sb, NT // G + 1)
                    act.dma_start(src_d, fT[0:H, :]).then_inc(src_out, 16)
                    act.wait_ge(ph, 3)
                    act.activation(ee[:, :, :, 0:1].rearrange("p t h o -> p t (h o)"), dd[:], ACT.Exp, bias=lgs[:]).then_inc(ph_act, 1)
                    act.activation(ee[:, :, :, 1:2].rearrange("p t h o -> p t (h o)"), dd[:], ACT.Exp, bias=lgs[:], scale=SLOPE).then_inc(ph_act, 1)
                    act.wait_ge(ph, 8)
                    act.activation(pos_w[:], pos_w[:], ACT.Exp).then_inc(ph_act, 1)
                    act.activation(neg_w[:], neg_w[:], ACT.Exp).then_inc(ph_act, 1)
                    with act.Fori(0, NT // G) as g:
                        for k in range(G):
                            i = k % 2
                            t1 = g * G + k + 1
                            act.wait_ge(t_made, (g * G + k) * 3 + 3)
                            act.wait_ge(uw_out[i], (g * 2 + k // 2) * 16 + 16)
                            act.activation(uws[:, i, :, 0:UW], tw[:, i].rearrange("p h k f -> p h (k f)"), ACT.Copy).then_inc(uw_hi, 1)
                            act.wait_ge(uw_lo, t1 + 2)
                            act.dma_start(
                                uw_d[:, :, bass.ds(g * G + k, 1), :].rearrange("h p o c -> p h (o c)"), uws[:, i]
                            ).then_inc(uw_out[i], 16)
                    for i in range(2):
                        act.wait_ge(kT_out[i], 16 * (NT // G + 1))
                        act.wait_ge(uw_out[i], 16 * (NT // 2 + 1))
                    act.wait_ge(src_out, 16)

                @block.tensor
                def _(pe):
                    pe.sem_inc(x_used, G)
                    pe.sem_inc(kT_ps, 2)
                    pe.sem_inc(m_used, 1)
                    pe.wait_ge(ids, 5)
                    with pe.Fori(0, NT // G) as g:
                        for k in range(G):
                            i = k % 2
                            t1 = g * G + k + 1
                            pe.wait_ge(x_in[k], g * 16 + 16)
                            pe.wait_ge(xT_sb, t1)
                            for c in range(C):
                                last = nc.tensor.transpose(psT[i][:, c * P : (c + 1) * P], x_s[:, k, c * P : (c + 1) * P], ident[:])
                            last.then_inc(xT_ps, 1)
                            pe.wait_ge(klo, t1 + 2)
                            pe.wait_ge(kT_sb, t1)
                            for h in range(H):
                                last = nc.tensor.transpose(psK[i][:, h, :], kk[:, i, h, :, :].rearrange("p k f -> p (k f)"), ident16[:])
                            last.then_inc(kT_ps, 1)
                            pe.wait_ge(xT_ps, t1)
                            pe.sem_inc(x_used, 1)
                        pe.wait_ge(xT_sb, g * G + G + 2)
                        pe.wait_ge(fT_sb, g + 1)
                        pe.wait_ge(w_lo, 2)
                        for c in range(C):
                            for wk, xk in HALVES:
                                last = nc.tensor.matmul(
                                    psF[0 : 2 * H, :], Wah[:, wk, c, :], xT[:, xk, c, bass.ds(g * 512, 512)],
                                    start=(c == 0 and wk == xk), stop=(c == C - 1 and xk == 1),
                                )
                        last.then_inc(fT_ps, 1)
                    pe.wait_ge(fT_sb, NT // G + 1)
                    for t in range(NT):
                        last = nc.tensor.transpose(psD[:, t, :], fT[:, t * P : (t + 1) * P], ident[0 : 2 * H, 0 : 2 * H])
                    last.then_inc(d_ps, 1)
                    with pe.Fori(0, NT // G) as g:
                        for k in range(G):
                            i = k % 2
                            pe.wait_ge(hp_used, g * G + k + 1)
                            for c in range(C):
                                for wk, xk in HALVES:
                                    last = nc.tensor.matmul(
                                        psH[i][:], xT[:, xk, c, bass.ds((g * G + k) * P, P)], Wh[:, wk, c, :],
                                        start=(c == 0 and wk == xk), stop=(c == C - 1 and xk == 1),
                                    )
                            last.then_inc(hp_ps, 1)
                            if k % 2 == 0:
                                half = k // 2
                                if half == 0:
                                    pe.wait_ge(m_conv, g + 2)
                                pe.wait_ge(m_sb, g * 2 + half + 1)
                                for t in range(2):
                                    for s in range(SUB):
                                        last = nc.tensor.transpose(psM[:, t, s, :], adj_f[:, s, (half * 2 + t) * P : (half * 2 + t + 1) * P], identb[:])
                                last.then_inc(m_ps, 1)
                                if half == 1:
                                    pe.wait_ge(m_ps, g * 2 + 2)
                                    pe.sem_inc(m_used, 1)

        with ExitStack() as main:
            nmT = sb(main, "nmT", [P, NT, IB], BF16)
            adj_s = sb(main, "adj_s", [P, SUB, IB], I32)
            adj_n = sb(main, "adj_n", [P, SUB, IB], BF16)
            uw = sb(main, "uw", [P, 2, NT, 2 * UW], F16)
            src_bc = sb(main, "src_bc", [P, 2, IB], F32)
            dst_h = sb(main, "dst_h", [P, 2, NT], F32)
            dst_neg = sb(main, "dst_neg", [P, 2, 2], F32)
            wall = sb(main, "wall", [P, 2, SUB, F1], F32)
            fac = sb(main, "fac", [P, 2, SUB, H], F32)
            rden = sb(main, "rden", [P, SUB], F32)
            elu = sb(main, "elu", [P, SUB, F], F32)
            X = sb(main, "X", [P, SUB, D], F32)
            O = sb(main, "O", [P, SUB, D], F32)
            E = sb(main, "E", [P, 2, 1024], F32)
            qq = sb(main, "qq", [P, SUB, H, 3, F], F16)
            masks = qq[:].rearrange("p s h k f -> p (s h k f)").bitcast(BF16)
            mpos = masks[:, 0 : RING * 2 * IB].rearrange("p (r n) -> p r n", r=RING)
            steps = sb(main, "steps", [P, 3, 2, IB], BF16)
            mneg = E[:].rearrange("p a b -> p (a b)").bitcast(BF16)[:, 0 : RING * 2 * IB].rearrange("p (r n) -> p r n", r=RING)
            qT = sb(main, "qT", [P, 2, 2, IB], F16)
            phi = sb(main, "phi", [P, 2, 1024], F16)
            plo = sb(main, "plo", [P, 2, 1024], F16)
            t1_ = phi[:].rearrange("p i n -> p (i n)").bitcast(F32)[:, 0 : SUB * F1].rearrange("p (s f) -> p s f", s=SUB)
            t2_ = plo[:].rearrange("p i n -> p (i n)").bitcast(F32)[:, 0 : SUB * F1].rearrange("p (s f) -> p s f", s=SUB)
            kT = sb(main, "kT", [P, 2, N], F16)
            vs = sb(main, "vs", [P, 2, NT, 2 * F1], F16)
            stats = sb(main, "stats", [P, SUB, 6], F32)
            mv = sb(main, "mv", [P, SUB, 2], F32)
            rstd = sb(main, "rstd", [P, SUB], F32)
            mhalf = sb(main, "mhalf", [P, SUB], F32)
            phalf = sb(main, "phalf", [P, H], F32)
            qn2 = sb(main, "qn2", [P, SUB, H], F32)
            qm = sb(main, "qm", [P, H], F32)
            qam = sb(main, "qam", [P, H], F32)
            qk2 = sb(main, "qk2", [P, H], F32)
            shift = sb(main, "shift", [P, H], F32)
            shift_h = sb(main, "shift_h", [P, 2, 1], F32)
            Ef = E[:].rearrange("p a b -> p (a b)")
            Xf = X[:].rearrange("p s d -> p (s d)")
            Of = O[:].rearrange("p s d -> p (s d)")

            ps_all = ps(main, "ps_all", [P, 8, 512], F32)
            psU = [ps_all[:, 2 * i : 2 * i + 2, 0 : 2 * UW].rearrange("p b (s c) -> p b s c", s=2) for i in range(2)]
            psW = [ps_all[:, 4 + i, 0 : SUB * F1].rearrange("p (s c) -> p s c", s=SUB) for i in range(2)]
            psS = [ps_all[:, 2 * i : 2 * i + 2, :].rearrange("p b n -> p (b n)") for i in range(2)]
            psO = psW
            psA = ps_all[:, 6, :].bitcast(BF16).rearrange("p (t s n) -> p t s n", t=2, s=SUB)
            psQ = ps_all[:, 7, :].bitcast(F16).rearrange("p (k n) -> p k n", k=2)

            adj_in = sem(main, "adj_in")
            adj_free = sem(main, "adj_free")
            adjn_ready = sem(main, "adjn_ready")
            adjn_read = sem(main, "adjn_read")
            adjps_ready = sem(main, "adjps_ready")
            adjT_ready = sem(main, "adjT_ready")
            x_in2 = sem(main, "x_in2")
            x_free2 = sem(main, "x_free2")
            x_less1 = sem(main, "x_less1")
            uw_in = [sem(main, f"uw_in{i}") for i in range(2)]
            src_in = [sem(main, f"src_in{i}") for i in range(2)]
            dst_ready = sem(main, "dst_ready")
            step_ready = sem(main, "step_ready")
            mpos_made = sem(main, "mpos_made")
            mneg_made = sem(main, "mneg_made")
            mask_used = sem(main, "mask_used")
            wall_ready = sem(main, "wall_ready")
            gat_out = sem(main, "gat_out")
            elu_exp = sem(main, "elu_exp")
            gat_chain = sem(main, "gat_chain")
            elu_chain = sem(main, "elu_chain")
            fac_ready = sem(main, "fac_ready")
            nm_ready = sem(main, "nm_ready")
            mid = sem(main, "mid")
            var_ready = sem(main, "var_ready")
            var_eps = sem(main, "var_eps")
            rstd_ready = sem(main, "rstd_ready")
            x1_ready = sem(main, "x1_ready")
            q_hi = sem(main, "q_hi")
            q_lo = sem(main, "q_lo")
            qn_ready = sem(main, "qn_ready")
            qn_all = sem(main, "qn_all")
            qk_ready = sem(main, "qk_ready")
            qk_root = sem(main, "qk_root")
            shift_ready = sem(main, "shift_ready")
            shh_ready = sem(main, "shh_ready")
            qps_ready = sem(main, "qps_ready")
            qT_ready = sem(main, "qT_ready")
            kT_in = [sem(main, f"kT_in{i}") for i in range(2)]
            v_in2 = [sem(main, f"v_in2{i}") for i in range(2)]
            s_ready = sem(main, "s_ready")
            s_free = sem(main, "s_free")
            e_ready = sem(main, "e_ready")
            phi_ready = sem(main, "phi_ready")
            phi_dve = sem(main, "phi_dve")
            plo_done = sem(main, "plo_done")
            pv_done = sem(main, "pv_done")
            att_head = sem(main, "att_head")
            att_out = sem(main, "att_out")
            att_chain = sem(main, "att_chain")
            last_chain = sem(main, "last_chain")
            y_ready = sem(main, "y_ready")
            out_done = sem(main, "out_done")
            consts = sem(main, "consts")
            pool_held2 = sem(main, "pool_held2")
            dve_held = sem(main, "dve_held")

            HP = H // 2

            with nc.Block() as block:

                @block.sync
                def _(sp):
                    def gat_loads(b, pair):
                        for i in range(2):
                            h = pair * 2 + i
                            sp.wait_ge(mask_used, (b * H + h + 1) * PAIRS + RING)
                            sp.dma_start(uw[:, i], uw_d[bass.ds(h, 1)].rearrange("o p t c -> p (o t) c")).then_inc(uw_in[i], 16)
                            sp.dma_start(
                                src_bc[:, i, :], src_d[bass.ds(h, 1), bass.ds(b * IB, IB)].rearrange("o n -> (o n)").partition_broadcast(P)
                            ).then_inc(src_in[i], 16)

                    def att_loads(b, nb):
                        with sp.Fori(0, HP) as hp:
                            for i in range(2):
                                h = hp * 2 + i
                                sp.wait_ge(adj_free, b * H + h + 1)
                                sp.dma_start(
                                    adj_s[:], adj_b[bass.ds(nb, 1), :, :, bass.ds(h * IB, IB)].rearrange("o p s j -> p (o s) j")
                                ).then_inc(adj_in, 16)
                                sp.wait_ge(att_head, b * H + h + 1)
                                sp.dma_start(kT[:, i, :], kT_d[bass.ds(h, 1)].rearrange("o p n -> p (o n)")).then_inc(kT_in[i], 16)
                                sp.dma_start(vs[:, i], v_d[bass.ds(h, 1)].rearrange("o p t c -> p (o t) c")).then_inc(v_in2[i], 16)

                    def store(b):
                        sp.wait_ge(y_ready, b + 1)
                        sp.dma_start(out_b[bass.ds(b, 1)].rearrange("o p s d -> p (o s) d"), O[:]).then_inc(out_done, 16)

                    gat_loads(0, 0)
                    with sp.Fori(0, NB - 1) as b:
                        with sp.Fori(1, HP) as hp:
                            gat_loads(b, hp)
                        att_loads(b, b + 1)
                        gat_loads(b + 1, 0)
                        store(b)
                    with sp.Fori(1, HP) as hp:
                        gat_loads(NB - 1, hp)
                    att_loads(NB - 1, NB - 1)
                    store(NB - 1)
                    sp.wait_ge(out_done, 16 * NB + 16)

                @block.gpsimd
                def _(pool):
                    def hold(semaphore, value):
                        pool.wait_ge(semaphore, value)
                        pool.sem_inc(pool_held2, 1)

                    nc.gpsimd.memset(mhalf[:], -0.5).then_inc(consts, 1)
                    nc.gpsimd.memset(phalf[:], 0.5).then_inc(consts, 1)
                    pool.sem_inc(adj_free, 1)
                    pool.sem_inc(x_free2, 1)

                    def rstd_step(n):
                        hold(var_ready, n + 1)
                        nc.gpsimd.tensor_scalar(rstd[:], mv[:, :, 1], EPS, None, ALU.add).then_inc(var_eps, 1)
                        pool.wait_ge(var_eps, n + 1)
                        nc.gpsimd.tensor_tensor(rstd[:], rstd[:], mhalf[:], ALU.pow).then_inc(rstd_ready, 1)

                    pool.wait_ge(consts, 2)
                    with pool.Fori(0, NB) as b:
                        hold(x_free2, b + 1)
                        pool.dma_start(X[:], x_b[bass.ds(b, 1)].rearrange("o p s d -> p (o s) d")).then_inc(x_in2, 16)
                        hold(x_in2, b * 16 + 16)
                        nc.gpsimd.tensor_scalar(Xf, Xf, -1.0, None, ALU.add).then_inc(x_less1, 1)
                        rstd_step(b * 2)
                        hold(qn_ready, b + 1)
                        nc.gpsimd.partition_all_reduce(qam[:], qm[:], P, RMAX).then_inc(qn_all, 1)
                        hold(qn_all, b + 1)
                        nc.gpsimd.tensor_tensor(qk2[:], qam[:], kmax2[:], ALU.mult).then_inc(qk_ready, 1)
                        hold(qk_ready, b + 1)
                        nc.gpsimd.tensor_tensor(qk2[:], qk2[:], phalf[:], ALU.pow).then_inc(qk_root, 1)
                        with pool.Fori(0, H) as st:
                            done = b * H + st
                            hold(adj_in, done * 16 + 16)
                            hold(adjn_read, done + 1)
                            nc.gpsimd.tensor_scalar(adj_n[:], adj_s[:], 0.0, None, ALU.is_gt).then_inc(adjn_ready, 1)
                            hold(adjn_ready, done + 1)
                            pool.sem_inc(adj_free, 1)
                        rstd_step(b * 2 + 1)

                def neg_count(p):
                    return p // 2

                def step_slot(p):
                    return (p - (p > DIRECT)) % 3

                @block.tensor
                def _(pe):
                    for s_, n_ in ((mask_used, 2 * PAIRS + RING), (adjn_read, 1), (att_head, 2), (pv_done, 2)):
                        pe.sem_inc(s_, n_)

                    def adj_half(done, half):
                        if half == 0:
                            pe.wait_ge(adjn_ready, done + 1)
                        pe.wait_ge(adjT_ready, 2 * H + done * 2 + half + 1)
                        for t in range(2):
                            for s in range(SUB):
                                last = nc.tensor.transpose(psA[:, t, s, :], adj_n[:, s, (half * 2 + t) * P : (half * 2 + t + 1) * P], identb[:])
                        last.then_inc(adjps_ready, 1)
                        if half == 1:
                            pe.wait_ge(adjps_ready, done * 2 + 2)
                            pe.sem_inc(adjn_read, 1)

                    def q_step(b, h):
                        pe.wait_ge(qT_ready, b * H + h + 1)
                        for kind in range(2):
                            for s in range(SUB):
                                last = nc.tensor.transpose(
                                    psQ[:, kind, s * P : (s + 1) * P],
                                    qq[:, s, bass.ds(h, 1), kind : kind + 2, :].rearrange("p o k f -> p (o k f)"),
                                    ident16[:],
                                )
                        last.then_inc(qps_ready, 1)

                    def head_ready(b, pair, i):
                        pe.wait_ge(kT_in[i], (b * HP + pair) * 16 + 16)
                        pe.wait_ge(v_in2[i], (b * HP + pair) * 16 + 16)
                        pe.wait_ge(qT_ready, b * H + pair * 2 + i + 2)

                    def scores(b, pair, i, g):
                        pe.wait_ge(s_free, (b * H + pair * 2 + i) * GROUPS + g + 1)
                        if g % 4 == 0:
                            pe.wait_ge(nm_ready, b * 4 + g // 4 + 1)
                        for t in range(2):
                            jt = 2 * g + t
                            dst = psS[g % 2][:, t * IB : (t + 1) * IB]
                            for kind in range(2):
                                nc.tensor.matmul(dst, kT[:, i, jt * P : (jt + 1) * P], qT[:, i, kind, :], start=(kind == 0), stop=False)
                            last = nc.tensor.matmul(dst, maskI[:], nmT[:, jt, :], start=False, stop=True)
                        last.then_inc(s_ready, 1)

                    def weigh(b, pair, i, g):
                        pe.wait_ge(plo_done, (b * H + pair * 2 + i) * GROUPS + g + 1 + 2)
                        for t in range(2):
                            jt = 2 * g + t
                            for s in range(SUB):
                                at = slice(t * IB + s * P, t * IB + (s + 1) * P)
                                for w, half in ((phi, 0), (phi, 1), (plo, 0)):
                                    last = nc.tensor.matmul(
                                        psO[i][:, s, :], w[:, g % 2, at], vs[:, i, jt, half * F1 : (half + 1) * F1],
                                        start=(jt == 0 and s == 0 and w is phi and half == 0), stop=(jt == NT - 1), skip_group_check=True,
                                    )
                        last.then_inc(pv_done, 1)

                    def att_pair(b, pair, last_pair):
                        for i in range(2):
                            h = pair * 2 + i
                            hb = b * H + h
                            final = last_pair and i == 1
                            pe.wait_ge(att_out, hb + 1)
                            for g in range(GROUPS):
                                if g + 2 < GROUPS:
                                    scores(b, pair, i, g + 2)
                                elif not final:
                                    after = (pair, 1) if i == 0 else (pair + 1, 0)
                                    if g + 2 == GROUPS:
                                        head_ready(b, *after)
                                    scores(b, *after, g + 2 - GROUPS)
                                weigh(b, pair, i, g)
                                if g == 3:
                                    adj_half(hb, 0)
                                if g == 7:
                                    adj_half(hb, 1)
                                if g == 8 and not final:
                                    q_step(b, h + 1)
                            pe.wait_ge(pv_done, hb * GROUPS + GROUPS + 2)
                            pe.sem_inc(att_head, 1)

                    with pe.Fori(0, NB) as b:
                        with pe.Fori(0, HP) as hp:
                            for i in range(2):
                                hb = b * H + hp * 2 + i
                                pe.wait_ge(uw_in[i], (b * HP + hp) * 16 + 16)
                                pe.wait_ge(gat_out, hb + 1)
                                for p in range(PAIRS):
                                    split = p % 2 == 1
                                    pe.wait_ge(mpos_made, hb * PAIRS + p + 1 + 3)
                                    for t in range(2):
                                        for s in range(SUB):
                                            at = slice(t * IB + s * P, t * IB + (s + 1) * P)
                                            cols = F1 if split else UW
                                            for half in range(2):
                                                last = nc.tensor.matmul(
                                                    psU[i][:, s // 2, s % 2, 0:cols], mpos[:, p % RING, at],
                                                    uw[:, i, 2 * p + t, half * UW : half * UW + cols],
                                                    start=(p == 0 and t == 0 and s % 2 == 0 and half == 0), stop=(p == PAIRS - 1), skip_group_check=True,
                                                )
                                    if split:
                                        pe.wait_ge(mneg_made, hb * SPLIT + neg_count(p) + 1)
                                    for t in range(2):
                                        for s in range(SUB):
                                            at = slice(t * IB + s * P, t * IB + (s + 1) * P)
                                            rest = mneg[:, p % RING, at] if split else adjT[:, 2 * p + t, s * P : (s + 1) * P]
                                            for half in range(2):
                                                last = nc.tensor.matmul(
                                                    psW[i][:, s, :], rest, uw[:, i, 2 * p + t, half * UW + F1 : half * UW + 2 * F1],
                                                    start=(p == 0 and t == 0 and s == 0 and half == 0), stop=(p == PAIRS - 1), skip_group_check=True,
                                                )
                                    last.then_inc(mask_used, 1)
                        pe.wait_ge(q_lo, b + 1)
                        q_step(b, 0)
                        head_ready(b, 0, 0)
                        scores(b, 0, 0, 0)
                        scores(b, 0, 0, 1)
                        with pe.Fori(0, HP - 1) as hp:
                            att_pair(b, hp, False)
                        att_pair(b, HP - 1, True)

                @block.scalar
                def _(act):
                    for s_, n_ in ((s_free, 2), (qT_ready, 1)):
                        act.sem_inc(s_, n_)

                    def wall_copy(b, h, i):
                        hb = b * H + h
                        act.wait_ge(mask_used, (hb + 3) * PAIRS + RING)
                        act.wait_ge(gat_out, hb + 1)
                        act.activation(wall[:, i], psW[i], ACT.Copy).then_inc(wall_ready, 1)

                    def elu_part(b, h):
                        act.wait_ge(gat_out, b * H + h + 1 + 2)
                        act.wait_ge(elu_chain, (b * H + h) * 2 + 2)
                        act.activation(elu[:], O[:, :, bass.ds(h * F, F)], ACT.Exp).then_inc(elu_exp, 1)

                    def dst_load(b, h, i):
                        act.activation(dst_h[:, i, :], dst_up[:, :, bass.ds(h, 1)].rearrange("p t o -> p (t o)"), ACT.Copy).then_inc(dst_ready, 1)
                        act.activation(
                            dst_neg[:, i, :], dst_up[:, 2 * DIRECT : 2 * DIRECT + 2, bass.ds(h, 1)].rearrange("p t o -> p (t o)"), ACT.Copy, scale=-1.0 / STEP_UP
                        ).then_inc(dst_ready, 1)

                    def gat_steps(b, h, i, pair, after, last_head=False):
                        hb = b * H + h
                        act.wait_ge(dst_ready, hb * 2 + 2)
                        act.wait_ge(src_in[i], (b * HP + pair) * 16 + 16)
                        for p in range(PAIRS):
                            if p != DIRECT:
                                act.wait_ge(mpos_made, hb * PAIRS + p + 1)
                                for t in range(2):
                                    last = act.activation(
                                        steps[:, step_slot(p), t, :], src_bc[:, i, :], ACT.Relu, bias=dst_h[:, i, 2 * p + t : 2 * p + t + 1], scale=STEP_UP
                                    )
                                last.then_inc(step_ready, 1)
                            if after and p == 5:
                                wall_copy(b, h - 1, 1 - i)
                            if after and p == 13:
                                elu_part(b, h - 1)
                            if p == 14 and not last_head:
                                dst_load(b, h + 1, 1 - i)

                    def q_copy(b, h, i):
                        act.wait_ge(qps_ready, b * H + h + 1)
                        act.activation(qT[:, i], psQ[:], ACT.Copy).then_inc(qT_ready, 1)

                    def att_pair(b, pair, last_pair):
                        for i in range(2):
                            h = pair * 2 + i
                            hb = b * H + h
                            act.activation(shift_h[:, i, :], shift[:, bass.ds(h, 1)], ACT.Copy).then_inc(shh_ready, 1)
                            act.wait_ge(shh_ready, hb + 1)
                            for g in range(GROUPS):
                                n = hb * GROUPS + g
                                act.wait_ge(s_ready, n + 1)
                                act.wait_ge(plo_done, n + 1)
                                act.activation(E[:, g % 2, :], psS[g % 2], ACT.Exp, bias=shift_h[:, i, :]).then_inc(e_ready, 1)
                                if g % 2 == 1:
                                    act.wait_ge(pv_done, n + 1)
                                    act.activation(phi[:, 1, :], psS[1], ACT.Exp, bias=shift_h[:, i, :]).then_inc(phi_ready, 1)
                                    act.wait_ge(phi_ready, hb * (GROUPS // 2) + g // 2 + 1)
                                else:
                                    act.wait_ge(e_ready, n + 1)
                                act.sem_inc(s_free, 1)
                                if g == 10 and not (last_pair and i == 1):
                                    q_copy(b, h + 1, 1 - i)

                    with act.Fori(0, NB) as b:
                        dst_load(b, 0, 0)
                        gat_steps(b, 0, 0, 0, False)
                        with act.Fori(0, HP - 1) as hp:
                            gat_steps(b, hp * 2 + 1, 1, hp, True)
                            gat_steps(b, hp * 2 + 2, 0, hp + 1, True)
                        gat_steps(b, H - 1, 1, HP - 1, True, last_head=True)
                        wall_copy(b, H - 1, 1)
                        elu_part(b, H - 1)
                        for s in range(SUB):
                            act.wait_ge(x1_ready, b * SUB + s + 1)
                            for k in (0, 2):
                                act.activation(qq[:, s, :, k, :], X[:, s, :].rearrange("p (h f) -> p h f", h=H), ACT.Copy, scale=SCALE).then_inc(q_hi, 1)
                        q_copy(b, 0, 0)
                        act.wait_ge(shift_ready, b + 1)
                        with act.Fori(0, HP - 1) as hp:
                            att_pair(b, hp, False)
                        att_pair(b, HP - 1, True)

                @block.vector
                def _(dve):
                    for s_, n_ in ((adjT_ready, 2 * H + 1), (gat_out, 2), (att_out, 2), (plo_done, 2), (out_done, 16), (mpos_made, 3), (elu_chain, 2)):
                        dve.sem_inc(s_, n_)

                    def gat_finish(b, h, i):
                        hb = b * H + h
                        a_pos = fac[:, 0, :, bass.ds(h, 1)].to_broadcast([P, SUB, F1])
                        a_neg = fac[:, 1, :, bass.ds(h, 1)].to_broadcast([P, SUB, F1])

                        def read_sums():
                            dve.wait_ge(wall_ready, hb + 1)
                            for bank in range(2):
                                rows = slice(2 * bank, 2 * bank + 2)
                                nc.vector.tensor_tensor(t1_[:, rows, :], wall[:, i, rows, :], psU[i][:, bank, :, F1:UW], ALU.subtract).then_inc(gat_chain, 1)
                                nc.vector.tensor_tensor(t2_[:, rows, :], psU[i][:, bank, :, 0:F1], a_pos[:, rows, :], ALU.mult).then_inc(gat_chain, 1)

                        def weigh_neg():
                            dve.wait_ge(gat_chain, hb * 7 + 4)
                            nc.vector.tensor_tensor(t1_[:], t1_[:], a_neg, ALU.mult).then_inc(gat_chain, 1)

                        def add():
                            dve.wait_ge(gat_chain, hb * 7 + 5)
                            nc.vector.tensor_tensor(t1_[:], t1_[:], t2_[:], ALU.add).then_inc(gat_chain, 1)

                        def invert():
                            dve.wait_ge(gat_chain, hb * 7 + 6)
                            nc.vector.reciprocal(rden[:], t1_[:, :, F]).then_inc(gat_chain, 1)

                        def divide():
                            dve.wait_ge(gat_chain, hb * 7 + 7)
                            dve.wait_ge(out_done, b * 16 + 16)
                            nc.vector.tensor_tensor(
                                O[:, :, bass.ds(h * F, F)], t1_[:, :, 0:F], rden[:].unsqueeze(2).to_broadcast([P, SUB, F]), ALU.mult
                            ).then_inc(gat_out, 1)

                        return [read_sums, weigh_neg, add, invert, divide]

                    def elu_add(b, h):
                        hb = b * H + h
                        at = bass.ds(h * F, F)
                        dve.wait_ge(elu_exp, hb + 1)
                        dve.wait_ge(x_less1, b + 1)
                        nc.vector.scalar_tensor_tensor(elu[:], elu[:], 1.0, X[:, :, at], ALU.min, ALU.add).then_inc(elu_chain, 1)
                        dve.wait_ge(elu_chain, hb * 2 + 1 + 2)
                        nc.vector.scalar_tensor_tensor(X[:, :, at], O[:, :, at], 0.0, elu[:], ALU.max, ALU.add).then_inc(elu_chain, 1)

                    def att_finish(b, h, i):
                        hb = b * H + h
                        dve.wait_ge(att_head, hb + 1 + 2)
                        nc.vector.reciprocal(rden[:], psO[i][:, :, F]).then_inc(att_chain, 1)
                        dve.wait_ge(att_chain, hb * 2 + 1)
                        nc.vector.tensor_tensor(
                            O[:, :, bass.ds(h * F, F)], psO[i][:, :, 0:F], rden[:].unsqueeze(2).to_broadcast([P, SUB, F]), ALU.mult
                        ).then_inc(att_chain, 1)
                        dve.wait_ge(att_chain, hb * 2 + 2)
                        dve.sem_inc(att_out, 1)

                    def norm_stats(rows, chain, base):
                        for s in range(SUB):
                            nc.vector.bn_stats(stats[:, s, :], rows[:, s, :]).then_inc(chain, 1)
                        dve.wait_ge(chain, base + SUB)
                        dve.sem_inc(dve_held, 1)
                        for s in range(SUB):
                            nc.vector.bn_aggr(mv[:, s, :], stats[:, s, :]).then_inc(chain, 1)
                        dve.wait_ge(chain, base + 2 * SUB)
                        dve.sem_inc(var_ready, 1)

                    def gat_masks(b, h, i, pair, hooks):
                        hb = b * H + h
                        dve.wait_ge(src_in[i], (b * HP + pair) * 16 + 16)
                        for p in range(PAIRS):
                            if p in hooks:
                                hooks[p]()
                            dve.wait_ge(mask_used, hb * PAIRS + p + 1 + 2 * PAIRS)
                            if p == DIRECT:
                                dve.wait_ge(dst_ready, hb * 2 + 2)
                                for t in range(2):
                                    last = nc.vector.scalar_tensor_tensor(
                                        mpos[:, p % RING, t * IB : (t + 1) * IB], src_bc[:, i, :], dst_neg[:, i, t : t + 1], adjT[:, 2 * p + t, :],
                                        ALU.is_gt, ALU.mult,
                                    )
                                last.then_inc(mpos_made, 1)
                            else:
                                dve.wait_ge(step_ready, hb * (PAIRS - 1) + p - (p > DIRECT) + 1)
                                nc.vector.tensor_tensor(
                                    mpos[:, p % RING, :], steps[:, step_slot(p)].rearrange("p t n -> p (t n)"), edges(p), ALU.min
                                ).then_inc(mpos_made, 1)
                            if p % 2 == 0 and p > 0:
                                others(hb, p - 1)
                        others(hb, PAIRS - 1)

                    def edges(p):
                        return adjT[:, 2 * p : 2 * p + 2, :].rearrange("p t n -> p (t n)")

                    def others(hb, p):
                        dve.wait_ge(mpos_made, hb * PAIRS + p + 1 + 3)
                        nc.vector.tensor_tensor(mneg[:, p % RING, :], edges(p), mpos[:, p % RING, :], ALU.subtract).then_inc(mneg_made, 1)

                    def finish_hooks(b, h, i):
                        hooks = {6 + n: finish for n, finish in enumerate(gat_finish(b, h, i))}
                        hooks[15] = lambda: elu_add(b, h)
                        return hooks

                    def first_head(b, hooks):
                        for k, w in ((0, pos_w), (1, neg_w)):
                            nc.vector.tensor_copy(fac[:, k], w[:, bass.ds(b * SUB, SUB), :]).then_inc(fac_ready, 1)
                        dve.wait_ge(fac_ready, b * 2 + 2)
                        dve.wait_ge(adjT_ready, (b + 1) * 2 * H + 1)
                        dve.wait_ge(plo_done, b * H * GROUPS + 2)
                        gat_masks(b, 0, 0, 0, hooks)

                    def att_groups(b, h, i, finish_before):
                        hb = b * H + h
                        for g in range(GROUPS):
                            n = hb * GROUPS + g
                            if g == 3 and finish_before:
                                att_finish(b, h - 1, 1 - i)
                            dve.wait_ge(e_ready, n + 1)
                            if g % 2 == 0:
                                dve.wait_ge(pv_done, n + 1)
                                nc.vector.tensor_copy(phi[:, 0, :], E[:, 0, :]).then_inc(phi_dve, 1)
                                dve.wait_ge(phi_dve, hb * (GROUPS // 2) + g // 2 + 1)
                            else:
                                dve.wait_ge(phi_ready, hb * (GROUPS // 2) + g // 2 + 1)
                            nc.vector.tensor_tensor(plo[:, g % 2, :], E[:, g % 2, :], phi[:, g % 2, :], ALU.subtract).then_inc(plo_done, 1)
                            for half, turn in ((0, 5), (1, 9)):
                                if g == turn:
                                    dve.wait_ge(adjps_ready, hb * 2 + half + 1)
                                    nc.vector.tensor_copy(
                                        adjT[:, bass.ds(h * 4 + half * 2, 2), :].rearrange("p t n -> p (t n)"), psA.rearrange("p t s n -> p (t s n)")
                                    ).then_inc(adjT_ready, 1)

                    def not_allowed(part):
                        rows = slice(part * NT // 4, (part + 1) * NT // 4)
                        nc.vector.tensor_scalar(
                            nmT[:, rows, :].rearrange("p t n -> p (t n)"), adjT[:, rows, :].rearrange("p t n -> p (t n)"), -1.0, 1.0, ALU.mult, ALU.add
                        ).then_inc(nm_ready, 1)

                    def after_first_head(b):
                        with dve.Fori(0, HP - 1) as hp:
                            gat_masks(b, hp * 2 + 1, 1, hp, finish_hooks(b, hp * 2, 0))
                            gat_masks(b, hp * 2 + 2, 0, hp + 1, finish_hooks(b, hp * 2 + 1, 1))
                        gat_masks(b, H - 1, 1, HP - 1, finish_hooks(b, H - 2, 0))
                        not_allowed(0)
                        for finish in gat_finish(b, H - 1, 1):
                            finish()
                        elu_add(b, H - 1)
                        dve.wait_ge(elu_chain, (b * H + H) * 2 + 2)
                        norm_stats(X, mid, b * 10)
                        not_allowed(1)
                        dve.wait_ge(rstd_ready, b * 2 + 1)
                        for s in range(SUB):
                            nc.vector.tensor_scalar(
                                X[:, s, :], X[:, s, :], mv[:, s, 0:1], rstd[:, s : s + 1], ALU.subtract, ALU.mult
                            ).then_inc(x1_ready, 1)
                        for s in range(SUB):
                            dve.wait_ge(q_hi, (b * SUB + s) * 2 + 2)
                            last = nc.vector.scalar_tensor_tensor(
                                qq[:, s, :, 1, :], X[:, s, :].rearrange("p (h f) -> p h f", h=H), SCALE, qq[:, s, :, 0, :], ALU.mult, ALU.subtract
                            )
                        last.then_inc(q_lo, 1)
                        nc.vector.tensor_tensor(Ef, Xf, Xf, ALU.mult).then_inc(mid, 1)
                        dve.wait_ge(mid, b * 10 + 9)
                        nc.vector.tensor_reduce(
                            qn2[:].rearrange("p s h -> p (s h)"), Ef.rearrange("p (n f) -> p n f", f=F), AX_X, ALU.add
                        ).then_inc(mid, 1)
                        dve.wait_ge(mid, b * 10 + 10)
                        nc.vector.tensor_reduce(qm[:], qn2[:].rearrange("p s h -> p h s"), AX_X, ALU.max).then_inc(qn_ready, 1)
                        not_allowed(2)
                        dve.wait_ge(qk_root, b + 1)
                        nc.vector.tensor_scalar(shift[:], qk2[:], -SCALE * 1.0001, LOG_ATT_SCALE, ALU.mult, ALU.add).then_inc(shift_ready, 1)
                        not_allowed(3)
                        att_groups(b, 0, 0, False)
                        with dve.Fori(0, HP - 1) as hp:
                            att_groups(b, hp * 2 + 1, 1, True)
                            att_groups(b, hp * 2 + 2, 0, True)
                        att_groups(b, H - 1, 1, True)

                    def last_sum(b):
                        att_finish(b, H - 1, 1)
                        nc.vector.tensor_tensor(Of, Of, Xf, ALU.add).then_inc(last_chain, 1)
                        dve.wait_ge(last_chain, b * 9 + 1)
                        dve.sem_inc(x_free2, 1)

                    def last_stats(b):
                        norm_stats(O, last_chain, b * 9 + 1)

                    def last_scale(b):
                        dve.wait_ge(rstd_ready, b * 2 + 2)
                        for s in range(SUB):
                            last = nc.vector.tensor_scalar(O[:, s, :], O[:, s, :], mv[:, s, 0:1], rstd[:, s : s + 1], ALU.subtract, ALU.mult)
                        last.then_inc(y_ready, 1)

                    first_head(0, {})
                    with dve.Fori(0, NB - 1) as b:
                        after_first_head(b)
                        first_head(b + 1, {2: lambda: last_sum(b), 4: lambda: last_stats(b), 8: lambda: last_scale(b)})
                    after_first_head(NB - 1)
                    last_sum(NB - 1)
                    last_stats(NB - 1)
                    last_scale(NB - 1)


_INS = ["x", "adj", "L0_gnn_W", "L0_gnn_a", "L1_gnn_x2", "L1_gnn_v"]


def kernel(**inputs):
    import numpy as _np
    import concourse.bacc as _bacc
    from concourse import mybir as _mybir
    from concourse.bass_utils import run_bass_kernel_spmd as _run

    nc = _bacc.Bacc("TRN2", target_bir_lowering=False, num_devices=1)
    arrays, args = {}, []
    for name in _INS:
        arr = _np.ascontiguousarray(inputs[name])
        arrays[f"in_{name}_dram"] = arr
        args.append(nc.dram_tensor(f"in_{name}_dram", arr.shape, _mybir.dt.from_np(arr.dtype), kind="ExternalInput").ap())
    shape = tuple(arrays["in_x_dram"].shape)
    args.append(nc.dram_tensor("out_0_dram", shape, _mybir.dt.float32, kind="ExternalOutput").ap())
    bass_gat_then_masked_attention(nc, *args)
    r = _run(nc, [arrays], core_ids=[0])
    return r.results[0]["out_0_dram"]
```
